# Optimizing a Trainium2 kernel written in Bass

```python
import numpy as np
import jax
import jax.numpy as jnp

def _softmax(x, axis=-1):
    return jax.nn.softmax(x, axis=axis)

def _gelu(x):
    return jax.nn.gelu(x, approximate=True)

def _silu(x):
    return jax.nn.silu(x)

def _sigmoid(x):
    return jax.nn.sigmoid(x)

def _layernorm(x, axis=-1, eps=1e-05):
    m = jnp.mean(x, axis=axis, keepdims=True)
    v = jnp.var(x, axis=axis, keepdims=True)
    return (x - m) / jnp.sqrt(v + eps)

def _scatter_add(tgt, idx, src, axis=0):
    return tgt.at[idx].add(src)

def _segment_sum(src, seg, n):
    return jax.ops.segment_sum(src, seg, n)
kernel_name = 'mk_xattn_seq_d1_seqx_r2_1ab7d9'

def setup_inputs(seed: int=0):
    np.random.seed(seed)
    _w = jnp.asarray

    def _rec_inputs():
        import jax
        import jax.numpy as jnp
        _rk = jax.random.key(seed)
        x = -0.000125 + 0.9999 * jax.random.normal(jax.random.fold_in(_rk, 1), (4, 1024, 1024), jnp.float32)
        _lenS = 1024 - jax.random.randint(jax.random.fold_in(_rk, 7), (4,), 0, max(1, 1024 // 4) + 1, jnp.int32)
        _lenS2 = 2048 - jax.random.randint(jax.random.fold_in(_rk, 8), (4,), 0, max(1, 2048 // 4) + 1, jnp.int32)
        _ctx_1024P = jax.random.normal(jax.random.fold_in(_rk, 11), (4, 16, 512), jnp.float32)
        _ctx_1024c = jax.random.dirichlet(jax.random.fold_in(_rk, 511), 0.3 * jnp.ones((16,), jnp.float32), (4, 2048))
        _ctx_1024t = jnp.einsum('bsk,bkd->bsd', _ctx_1024c, _ctx_1024P)
        _ctx_1024t = _ctx_1024t * jax.lax.rsqrt(jnp.mean(jnp.square(_ctx_1024t)) + 1e-12) * 0.953939
        ctx_1024 = 4.13588e-05 + 0.999923 * (_ctx_1024t + 0.3 * jax.random.normal(jax.random.fold_in(_rk, 611), (4, 2048, 512), jnp.float32))
        return (x, ctx_1024)
    x, ctx_1024 = _rec_inputs()

    def _L0_xattn_setup():
        import jax, jax.numpy as jnp
        import numpy as np
        EPS = 1e-06

        def _rmsnorm(x, w):
            var = jnp.mean(jnp.square(x), axis=-1, keepdims=True)
            return x * jax.lax.rsqrt(var + EPS) * w
        key = jax.random.key(seed)
        ks = jax.random.split(key, 6)
        B, N, M = (4, 2048, 1024)
        d_model, memory_dim = (1024, 512)
        hidden_states = jax.random.normal(ks[0], (B, N, d_model), dtype=jnp.float32)
        memory = jax.random.normal(ks[1], (B, M, memory_dim), dtype=jnp.float32)
        W_mem = jax.random.normal(ks[2], (d_model, memory_dim), dtype=jnp.float32) / np.sqrt(memory_dim)
        W_gate = jax.random.normal(ks[3], (d_model, 2 * d_model), dtype=jnp.float32) / np.sqrt(2 * d_model)
        b_gate = jax.random.normal(ks[4], (d_model,), dtype=jnp.float32) * 0.01
        norm_w = jnp.ones((d_model,), dtype=jnp.float32)
        return {'hidden_states': hidden_states, 'memory': memory, 'W_mem': W_mem, 'W_gate': W_gate, 'b_gate': b_gate, 'norm_w': norm_w}
    _L0_xattn_all = _L0_xattn_setup()
    _L0_xattn_in = {k: v for k, v in _L0_xattn_all.items() if k in ('W_mem', 'W_gate', 'b_gate', 'norm_w')}
    del _L0_xattn_all
    return {'x': x, 'ctx_1024': ctx_1024, 'L0_xattn_W_mem': _L0_xattn_in['W_mem'], 'L0_xattn_W_gate': _L0_xattn_in['W_gate'], 'L0_xattn_b_gate': _L0_xattn_in['b_gate'], 'L0_xattn_norm_w': _L0_xattn_in['norm_w']}

def reference(x, ctx_1024, L0_xattn_W_mem, L0_xattn_W_gate, L0_xattn_b_gate, L0_xattn_norm_w):
    import jax
    import jax.numpy as jnp

    def _L0_xattn_ref(hidden_states, memory, W_mem, W_gate, b_gate, norm_w):
        import jax, jax.numpy as jnp
        import numpy as np
        EPS = 1e-06

        def _rmsnorm(x, w):
            var = jnp.mean(jnp.square(x), axis=-1, keepdims=True)
            return x * jax.lax.rsqrt(var + EPS) * w
        D = hidden_states.shape[-1]
        memory_proj = jnp.einsum('bme,de->bmd', memory, W_mem)
        scores = jnp.einsum('bnd,bmd->bnm', hidden_states, memory_proj) / jnp.sqrt(jnp.float32(D))
        attn = jax.nn.softmax(scores, axis=-1)
        memory_context = jnp.einsum('bnm,bmd->bnd', attn, memory_proj)
        gate_input = jnp.concatenate([hidden_states, memory_context], axis=-1)
        gate = jax.nn.sigmoid(jnp.einsum('bnf,df->bnd', gate_input, W_gate) + b_gate)
        fused = hidden_states + gate * memory_context
        return _rmsnorm(fused, norm_w)
    x = _L0_xattn_ref(x, ctx_1024, L0_xattn_W_mem, L0_xattn_W_gate, L0_xattn_b_gate, L0_xattn_norm_w)
    return x

_drawn_inputs = setup_inputs


def setup_inputs(seed=0):
    import zlib

    import numpy as np

    out = dict(_drawn_inputs(seed))
    spreads = {'L0_xattn_norm_w': (1.0, 0.2)}
    factors = {'L0_xattn_b_gate': 50.71}
    for name, (base, spread) in spreads.items():
        noise = np.random.default_rng([zlib.crc32(name.encode()), seed]).standard_normal(out[name].shape)
        drawn = base * np.exp(spread * noise) if base else spread * noise
        out[name] = jnp.asarray(drawn.astype(out[name].dtype))
    for name, factor in factors.items():
        out[name] = (out[name] * factor).astype(out[name].dtype)
    return out
```

```python
from contextlib import ExitStack

import concourse.bass as bass
from concourse import mybir

ALU = mybir.AluOpType
ACT = mybir.ActivationFunctionType
AX_X = mybir.AxisListType.X
F32 = mybir.dt.float32
F32R = mybir.dt.float32r

P = 128
NQ = 4
SQ = 32
BANK = 512
HI, LO = 0, 1
PASSES = ((HI, HI), (HI, LO), (LO, HI))
RMS_EPS = 1e-6


def build(nc, x, mem, w_mem, w_gate, b_gate, norm_w, out):
    NB, N, D = x.shape
    _, M, C = mem.shape
    ROWS = NB * N
    NBLK = ROWS // BANK
    NUNIT = ROWS // P
    UPB = N // P
    DT = D // P
    CT = C // P
    MB = M // BANK
    TPB = BANK // P
    DH = D // BANK
    GB = D // BANK
    CHX = D // NQ
    CHC = C // NQ
    SCALE = float(D) ** -0.5
    assert C == BANK and M % BANK == 0 and MB == 4 and DT == 8 and UPB == 8 and DH == 2

    x_rows = x.rearrange("b n d -> (b n) d")
    out_rows = out.rearrange("b n d -> (b n) d")

    q_dram = nc.dram_tensor("q_scratch", [NUNIT, P, CT * 2 * P], F32).ap()
    am_dram = nc.dram_tensor("am_scratch", [NUNIT, P, TPB * CHC], F32).ap()
    wg1_dram = nc.dram_tensor("wg1_scratch", [P, DT, 2, D], F32).ap()
    wm_dram = nc.dram_tensor("wm_scratch", [P, CT, 2, D], F32).ap()
    wc_dram = nc.dram_tensor("wc_scratch", [P, CT, 2, D], F32).ap()

    with ExitStack() as ctx:
        def sb(name, shape, dt):
            return ctx.enter_context(nc.sbuf_tensor(name, shape, dt))

        def sem(name):
            return ctx.enter_context(nc.semaphore(name))

        KW = 256
        R1 = sb("region_t", [P, 64 * KW], F32R)
        R2 = sb("region_n", [P, 64 * KW], F32R)
        R3 = sb("region_l", [P, 20 * KW], F32R)
        F = sb("region_f", [P, 48 * KW], F32)
        prob = sb("prob", [P, M], F32)
        am_out = sb("am_out", [P, C], F32)
        ident = sb("ident", [P, P], F32)
        max_part = sb("max_part", [P, MB], F32)
        row_max = sb("row_max", [P, 1], F32)
        neg_max = sb("neg_max", [P, 1], F32)
        sum_part = sb("sum_part", [P, MB], F32)
        row_sum = sb("row_sum", [P, 1], F32)
        row_inv = sb("row_inv", [P, 1], F32)
        sq_sum = sb("sq_sum", [P, 1], F32)
        mean_sq = sb("mean_sq", [P, 1], F32)
        rstd = sb("rstd", [P, 1], F32)
        m_half = sb("minus_half", [P, 1], F32)

        a_wt = R1[:, 0:32 * KW]
        a_xt = R1[:, 32 * KW:64 * KW].rearrange("p (h t n) -> p h t n", h=2, t=DT)
        a_w = R2[:, 0:32 * KW].rearrange("p (h t c) -> p h t c", h=2, t=DT)
        a_q = R2[:, 32 * KW:48 * KW].rearrange("p (u c h n) -> p u c h n", u=TPB, c=CT, h=2)
        a_in = F[:, 0:16 * KW]
        a_tf = F[:, 16 * KW:32 * KW]
        a_wf = F[:, 32 * KW:48 * KW].rearrange("p (t c) -> p t c", t=DT)
        b_mt = R1[:, :].rearrange("p (j h t m) -> p j h t m", j=MB, h=2, t=CT)
        b_mn = R2[:, :].rearrange("p (j h s c) -> p j h s c", j=MB, h=2, s=TPB)
        b_pt = R3[:, 0:16 * KW].rearrange("p (h k n) -> p h k n", h=2, k=MB * TPB)
        b_q = R3[:, 16 * KW:20 * KW].rearrange("p (c h n) -> p c h n", c=CT, h=2)
        b_in = [F[:, 8 * KW * s:8 * KW * (s + 1)] for s in range(4)]
        b_tf = [F[:, 8 * KW * s:8 * KW * (s + 1)] for s in (4, 5)]
        c_wg1 = R1[:, :].rearrange("p (t h d) -> p t h d", t=DT, h=2)
        c_wc = R2[:, 0:32 * KW].rearrange("p (t h d) -> p t h d", t=CT, h=2)
        c_wm = R2[:, 32 * KW:64 * KW].rearrange("p (t h d) -> p t h d", t=CT, h=2)
        c_xt = [R3[:, 16 * KW:20 * KW], R3[:, 0:4 * KW]]
        c_at = [R3[:, 4 * KW:6 * KW], R3[:, 6 * KW:8 * KW]]
        c_xin, c_xtf, c_xres, c_z, c_u, c_out, c_bias, c_nw = (
            F[:, 4 * KW * s:4 * KW * (s + 1)] for s in range(8))
        c_ain, c_atf = (F[:, 32 * KW + 2 * KW * s:32 * KW + 2 * KW * (s + 1)] for s in range(2))
        c_sq = F[:, 36 * KW:40 * KW]

        bank = [ctx.enter_context(nc.psum_tensor(f"bank{i}", [P, BANK], F32)) for i in range(7)]
        ps_t = bank[4:6]
        ps_am = bank[6]
        ps_z, ps_c = bank[0:2], bank[2:4]

        const_zero, const_ready = sem("const_zero"), sem("const_ready")
        w_loaded, w_hi, w_ready = sem("w_loaded"), sem("w_hi"), sem("w_ready")
        item_loaded, item_t = sem("item_loaded"), sem("item_t")
        xt_hi, xt_ready = sem("xt_hi"), sem("xt_ready")
        wt_hi, wt_ready, wt_stored = sem("wt_hi"), sem("wt_ready"), sem("wt_stored")
        q_half, q_done = sem("q_half"), sem("q_done")
        q_hi, q_ready = sem("q_hi"), sem("q_ready")
        wc_stored, q_stored = sem("wc_stored"), sem("q_stored")
        mt_loaded = [sem(f"mt_loaded{j}") for j in range(MB)]
        mn_loaded = [sem(f"mn_loaded{j}") for j in range(MB)]
        mt_t, mt_hi, mt_ready = sem("mt_t"), sem("mt_hi"), sem("mt_ready")
        mn_hi, mn_ready = sem("mn_hi"), sem("mn_ready")
        uq_loaded = sem("uq_loaded")
        s_done, max_done, max_all, neg_ready = sem("s_done"), sem("max_done"), sem("max_all"), sem("neg_ready")
        exp_done, sum_done, inv_done = sem("exp_done"), sem("sum_done"), sem("inv_done")
        t_done, pt_hi, pt_ready = sem("t_done"), sem("pt_hi"), sem("pt_ready")
        av_done, am_ready, am_stored = sem("av_done"), sem("am_ready"), sem("am_stored")
        wg1_loaded = [sem(f"wg1_loaded{t}") for t in range(DT)]
        wc_loaded, wm_loaded, vec_loaded = sem("wc_loaded"), sem("wm_loaded"), sem("vec_loaded")
        xin_loaded, ain_loaded, xres_loaded = sem("xin_loaded"), sem("ain_loaded"), sem("xres_loaded")
        cx_t, cx_hi, cx_ready, cx_used = sem("cx_t"), sem("cx_hi"), sem("cx_ready"), sem("cx_used")
        ca_t, ca_hi, ca_ready = sem("ca_t"), sem("ca_hi"), sem("ca_ready")
        z_done, z_biased, gate_done = sem("z_done"), sem("z_biased"), sem("gate_done")
        c_done, mul_done, fused_done = sem("c_done"), sem("mul_done"), sem("fused_done")
        sq_done, var_done, rstd_done = sem("sq_done"), sem("var_done"), sem("rstd_done")
        out_ready, out_stored = sem("out_ready"), sem("out_stored")

        HEAD = ("G0", "G1", "E0", "X0", "E1", "X1", "E2", "X2")
        HEAD_BLOCKS = ("G0", "G1", "X0", "X1", "X2")
        NHB = len(HEAD_BLOCKS)
        NBLOCKS = GB + NBLK

        def item_of_x(n):
            return n + len(HEAD) - 3

        def load_quadrants(eng, dst, src, width, signal):
            chunk = width // NQ
            v = dst.rearrange("p (b f) -> p b f", f=chunk)
            for q in range(NQ):
                eng.dma_start(v[SQ * q:SQ * (q + 1)],
                              src[:, chunk * q:chunk * (q + 1)].rearrange("(b i) f -> i b f", i=SQ)
                              ).then_inc(signal, 16)

        def transpose_blocks(dst, src, tiles):
            return nc.vector.transpose(dst.rearrange("p (t b i) -> p t b i", t=tiles, i=SQ),
                                       src.rearrange("p (b t j) -> p t b j", t=tiles, j=SQ))

        def minus_hi(dst, src, hi):
            return nc.vector.tensor_tensor(dst, src, hi.bitcast(F32), ALU.subtract)

        block = ctx.enter_context(nc.Block())

        @block.sync
        def _(sp):
            for q in range(NQ):
                sp.dma_start(a_wf[SQ * q:SQ * (q + 1)],
                             w_mem[CHX * q:CHX * (q + 1), :].rearrange("(t j) c -> j t c", j=SQ)
                             ).then_inc(w_loaded, 16)

            def load_item(name, n):
                if n > 0:
                    sp.wait_ge(item_t, n)
                k = int(name[1])
                if name[0] == "G":
                    load_quadrants(sp, a_in, w_gate[BANK * k:BANK * (k + 1), D:2 * D], D, item_loaded)
                elif name[0] == "X":
                    load_quadrants(sp, a_in, x_rows[BANK * k:BANK * (k + 1), :], D, item_loaded)
                elif name == "E2":
                    load_quadrants(sp, a_in, w_mem, C, item_loaded)
                else:
                    load_quadrants(sp, a_in, w_gate[BANK * k:BANK * (k + 1), 0:D], D, item_loaded)

            def store_wt(e):
                sp.wait_ge(wt_ready, e + 1)
                if e < 2:
                    v = a_wt.bitcast(F32).rearrange("p (h t n) -> p t h n", h=2, t=DT)
                    for h in range(2):
                        sp.dma_start(wg1_dram[:, :, h, BANK * e:BANK * (e + 1)], v[:, :, h]).then_inc(wt_stored, 16)
                else:
                    v = a_wt.bitcast(F32).rearrange("p (h t n) -> p t h n", h=2, t=CT)
                    for h in range(2):
                        sp.dma_start(wm_dram[:, :, h, :], v[:, :, h]).then_inc(wt_stored, 16)

            def store_wc(k):
                sp.wait_ge(q_ready, CT * (k + 1))
                for u in range(TPB):
                    sp.dma_start(wc_dram[:, :, :, BANK * k + P * u:BANK * k + P * (u + 1)],
                                 a_q[:, u].bitcast(F32)).then_inc(wc_stored, 16)

            def store_q(n):
                sp.wait_ge(q_ready, (n + (GB + 1)) * CT)
                sp.dma_start(q_dram[bass.ds(n * TPB, TPB)].rearrange("u p f -> p u f"),
                             a_q.bitcast(F32).rearrange("p u c h n -> p u (c h n)")).then_inc(q_stored, 16)

            load_item("G0", 0)
            load_item("G1", 1)
            load_item("E0", 2)
            load_item("X0", 3)
            store_wt(0)
            store_wc(0)
            load_item("E1", 4)
            load_item("X1", 5)
            store_wt(1)
            store_wc(1)
            load_item("E2", 6)
            load_item("X2", 7)
            store_wt(2)
            store_q(0)
            with sp.Fori(3, NBLK) as n:
                sp.wait_ge(item_t, n + (len(HEAD) - 3))
                load_quadrants(sp, a_in, x_rows[bass.ds(n * BANK, BANK), :], D, item_loaded)
                store_q(n - 2)

            def load_mt(b, j):
                load_quadrants(sp, b_in[j], mem[b, BANK * j:BANK * (j + 1), :], C, mt_loaded[j])

            def load_mn(b, j):
                sp.dma_start(b_in[j].rearrange("p (s c) -> p s c", s=TPB),
                             mem[b, BANK * j:BANK * (j + 1), :].rearrange("(s p) c -> p s c", p=P)
                             ).then_inc(mn_loaded[j], 16)

            def load_q(unit):
                sp.dma_start(b_q.bitcast(F32).rearrange("p c h n -> p (c h n)"), q_dram[unit]).then_inc(uq_loaded, 16)

            def store_am(i):
                sp.wait_ge(am_ready, i + 1)
                v = am_dram[i].rearrange("(q i) (b c) -> b i q c", q=NQ, b=TPB)
                for b in range(TPB):
                    sp.dma_start(v[b], am_out[SQ * b:SQ * (b + 1), :].rearrange("i (q c) -> i q c", q=NQ)
                                 ).then_inc(am_stored, 16)

            sp.wait_ge(item_t, item_of_x(NBLK))
            load_mt(0, 0)
            load_mt(0, 1)
            store_q(NBLK - 2)
            sp.wait_ge(xt_ready, 2 * NBLOCKS)
            load_mt(0, 2)
            load_mt(0, 3)
            sp.wait_ge(mt_t, 2)
            load_mn(0, 0)
            load_mn(0, 1)
            store_q(NBLK - 1)
            sp.wait_ge(q_stored, 16 * NBLK)
            load_q(0)
            sp.wait_ge(mt_t, MB)
            load_mn(0, 2)
            load_mn(0, 3)
            sp.wait_ge(s_done, MB)
            load_q(1)

            def step_sp(i, unit_after_next=True):
                if unit_after_next:
                    sp.wait_ge(s_done, (i + 2) * MB)
                    load_q(i + 2)
                store_am(i)

            def load_next_mt(b):
                sp.wait_ge(mn_ready, (b + 1) * MB)
                for j in range(MB):
                    load_mt(b + 1, j)

            def load_next_mn(b, half):
                sp.wait_ge(mt_t, (b + 1) * MB + 2 * half + 2)
                for j in (2 * half, 2 * half + 1):
                    load_mn(b + 1, j)

            step_sp(0)
            with sp.Fori(0, NB - 1) as b:
                load_next_mt(b)
                with sp.Fori(1, 6) as u:
                    step_sp(b * UPB + u)
                load_next_mn(b, 0)
                sp.wait_ge(s_done, (b * UPB + 8) * MB)
                load_q(b * UPB + 8)
                load_next_mn(b, 1)
                store_am(b * UPB + 6)
                step_sp(b * UPB + 7)
                step_sp(b * UPB + 8)
            LB = (NB - 1) * UPB

            sp.wait_ge(mn_ready, NB * MB)
            sp.dma_start(c_bias, b_gate.rearrange("(a d) -> a d", a=1).to_broadcast([P, D])).then_inc(vec_loaded, 16)
            sp.dma_start(c_nw, norm_w.rearrange("(a d) -> a d", a=1).to_broadcast([P, D])).then_inc(vec_loaded, 16)
            sp.dma_start(c_xres, x_rows[0:P, :]).then_inc(xres_loaded, 16)
            load_quadrants(sp, c_xin, x_rows[0:P, :], D, xin_loaded)
            sp.wait_ge(am_stored, 64)
            sp.dma_start(c_ain, am_dram[0]).then_inc(ain_loaded, 16)
            with sp.Fori(1, 6) as u:
                step_sp(LB + u)
            sp.wait_ge(s_done, NUNIT * MB)
            sp.wait_ge(wt_stored, 3 * 32)
            for t in range(DT):
                sp.dma_start(c_wg1[:, t].bitcast(F32), wg1_dram[:, t]).then_inc(wg1_loaded[t], 16)
            store_am(NUNIT - 2)
            sp.wait_ge(av_done, NUNIT)
            sp.wait_ge(wc_stored, 2 * 64)
            for t in range(CT):
                sp.dma_start(c_wc[:, t].bitcast(F32), wc_dram[:, t]).then_inc(wc_loaded, 16)
            for t in range(CT):
                sp.dma_start(c_wm[:, t].bitcast(F32), wm_dram[:, t]).then_inc(wm_loaded, 16)
            store_am(NUNIT - 1)
            sp.wait_ge(am_stored, 64 * NUNIT)

            def load_inputs(k):
                sp.wait_ge(cx_t, k)
                load_quadrants(sp, c_xin, x_rows[bass.ds(k * P, P), :], D, xin_loaded)
                sp.wait_ge(ca_t, k)
                sp.dma_start(c_ain, am_dram[k]).then_inc(ain_loaded, 16)

            def store_out(k):
                sp.wait_ge(out_ready, k + 1)
                sp.dma_start(out_rows[bass.ds(k * P, P), :], c_out).then_inc(out_stored, 16)

            def next_residual(k):
                sp.wait_ge(fused_done, k + 1)
                sp.dma_start(c_xres, x_rows[bass.ds(k * P + P, P), :]).then_inc(xres_loaded, 16)

            load_inputs(1)
            with sp.Fori(0, NUNIT - 2) as k:
                load_inputs(k + 2)
                next_residual(k)
                store_out(k)
            next_residual(NUNIT - 2)
            store_out(NUNIT - 2)
            store_out(NUNIT - 1)
            sp.wait_ge(out_stored, 16 * NUNIT)

        @block.gpsimd
        def _(pool):
            nc.gpsimd.memset(m_half[:], -0.5).then_inc(const_zero, 1)
            nc.gpsimd.memset(ident[:], 0.0).then_inc(const_zero, 1)
            pool.wait_ge(const_zero, 2)
            nc.gpsimd.affine_select(out=ident[:], in_=ident[:], compare_op=ALU.not_equal, fill=1.0, base=0,
                                    pattern=[[-1, P]], channel_multiplier=1).then_inc(const_ready, 1)
            with pool.Fori(0, NUNIT) as k:
                pool.wait_ge(var_done, k + 1)
                nc.gpsimd.tensor_tensor(rstd[:], mean_sq[:], m_half[:], ALU.pow).then_inc(rstd_done, 1)

        @block.scalar
        def _(act):
            act.wait_ge(w_loaded, 16 * NQ)
            for c in range(CT):
                nc.scalar.copy(a_w[:, HI, :, P * c:P * (c + 1)].rearrange("p t (q j) -> p t q j", q=NQ),
                               a_wf.rearrange("p t (q c j) -> p t c q j", q=NQ, j=SQ)[:, :, c]).then_inc(w_hi, 1)

            def split_half(item, half):
                n = DT // 2 * BANK
                nc.scalar.copy(a_xt[:, HI, DT // 2 * half:DT // 2 * (half + 1), :].rearrange("p t n -> p (t n)"),
                               a_tf[:, n * half:n * (half + 1)]).then_inc(xt_hi, 1)

            def split_wt(e, item):
                act.wait_ge(item_t, item + 1)
                if e > 0:
                    act.wait_ge(wt_stored, 32 * e)
                nc.scalar.copy(a_wt[:, 0:16 * KW], a_tf).then_inc(wt_hi, 1)

            def evacuate_q(k, free):
                free()
                for c in range(CT):
                    act.wait_ge(q_done, k * CT + c + 1)
                    nc.scalar.copy(a_q[:, :, c, HI, :], bank[c][:].rearrange("p (u n) -> p u n", u=TPB)
                                   ).then_inc(q_hi, 1)

            act.wait_ge(item_t, 1)
            split_half(0, 0)
            split_half(0, 1)
            for k in range(NHB - 1):
                nxt = HEAD_BLOCKS[k + 1]
                item = HEAD.index(nxt)
                if HEAD[item - 1][0] == "E":
                    split_wt(int(HEAD[item - 1][1]), item - 1)
                act.wait_ge(item_t, item + 1)
                act.wait_ge(q_half, k + 1)
                split_half(item, 0)
                if k == 0:
                    evacuate_q(k, lambda: None)
                elif k <= GB:
                    evacuate_q(k, lambda: act.wait_ge(wc_stored, 64 * k))
                else:
                    evacuate_q(k, lambda: act.wait_ge(q_stored, 16 * (k - GB)))
                split_half(item, 1)
            with act.Fori(NHB - 1, NBLOCKS - 1) as k:
                act.wait_ge(item_t, k + (item_of_x(0) - GB) + 2)
                act.wait_ge(q_half, k + 1)
                split_half(None, 0)
                evacuate_q(k, lambda: act.wait_ge(q_stored, (k - GB) * 16))
                split_half(None, 1)

            def mt_split(b, j):
                act.wait_ge(mt_t, b * MB + j + 1)
                nc.scalar.copy(b_mt[:, j, HI].rearrange("p t m -> p (t m)"), b_tf[j % 2]).then_inc(mt_hi, 1)

            def mn_split(b, j):
                act.wait_ge(mn_loaded[j], (b + 1) * 16)
                nc.scalar.copy(b_mn[:, j, HI].rearrange("p s c -> p (s c)"), b_in[j]).then_inc(mn_hi, 1)

            def exps(unit):
                act.wait_ge(neg_ready, unit + 1)
                for j in range(MB):
                    nc.scalar.activation(prob[:, BANK * j:BANK * (j + 1)], bank[j][:], ACT.Exp, bias=neg_max[:],
                                         scale=SCALE, accum_out=sum_part[:, j:j + 1]).then_inc(exp_done, 1)

            def step_act(i, mn_of=None, mt_of=None, softmax=True, first=False):
                if mn_of is not None:
                    if first:
                        act.wait_ge(q_done, NBLOCKS * CT)
                    else:
                        act.wait_ge(av_done, mn_of * UPB)
                for g in range(MB):
                    if mn_of is not None:
                        mn_split(mn_of, g)
                    act.wait_ge(t_done, i * MB + g + 1)
                    nc.scalar.copy(b_pt[:, HI, TPB * g:TPB * (g + 1), :].rearrange("p k n -> p (k n)"),
                                   ps_t[g % 2][:]).then_inc(pt_hi, 1)
                if mt_of is not None:
                    act.wait_ge(s_done, (mt_of * UPB) * MB)
                    mt_split(mt_of, 0)
                    mt_split(mt_of, 1)
                if softmax:
                    act.wait_ge(sum_done, i + 1)
                    exps(i + 1)
                if mt_of is not None:
                    mt_split(mt_of, 2)
                    mt_split(mt_of, 3)

            act.wait_ge(wt_stored, 32 * 3)
            mt_split(0, 0)
            mt_split(0, 1)
            evacuate_q(NBLOCKS - 1, lambda: act.wait_ge(q_stored, 16 * (NBLK - 1)))
            mt_split(0, 2)
            mt_split(0, 3)
            exps(0)
            act.wait_ge(q_stored, 16 * NBLK)
            step_act(0, mn_of=0, first=True)
            with act.Fori(0, NB - 1) as b:
                with act.Fori(1, 6) as u:
                    step_act(b * UPB + u)
                step_act(b * UPB + 6, mt_of=b + 1)
                step_act(b * UPB + 7)
                step_act(b * UPB + 8, mn_of=b + 1)
            LB = (NB - 1) * UPB
            with act.Fori(1, 7) as u:
                step_act(LB + u)
            step_act(LB + 7, softmax=False)

            def split_x(k):
                act.wait_ge(cx_t, k + 1)
                nc.scalar.copy(c_xt[HI], c_xtf).then_inc(cx_hi, 1)

            def split_am(k):
                act.wait_ge(ca_t, k + 1)
                nc.scalar.copy(c_at[HI], c_atf).then_inc(ca_hi, 1)

            def unit_act(k, following=True):
                if following:
                    act.wait_ge(cx_used, k + 1)
                    split_x(k + 1)
                for h in range(DH):
                    act.wait_ge(z_biased, k * DH + h + 1)
                    v = c_z[:, BANK * h:BANK * (h + 1)]
                    nc.scalar.activation(v, v, ACT.Sigmoid).then_inc(gate_done, 1)
                if following:
                    act.wait_ge(c_done, k * DH + DH)
                    split_am(k + 1)
                act.wait_ge(fused_done, k + 1)
                nc.scalar.activation(c_sq, c_u, ACT.Square, accum_out=sq_sum[:]).then_inc(sq_done, 1)

            split_x(0)
            act.wait_ge(av_done, NUNIT)
            split_am(0)
            with act.Fori(0, NUNIT - 1) as k:
                unit_act(k)
            unit_act(NUNIT - 1, following=False)

        @block.vector
        def _(dve):
            for c in range(CT):
                dve.wait_ge(w_hi, c + 1)
                minus_hi(a_w[:, LO, :, P * c:P * (c + 1)].rearrange("p t (q j) -> p t q j", q=NQ),
                         a_wf.rearrange("p t (q c j) -> p t c q j", q=NQ, j=SQ)[:, :, c],
                         a_w[:, HI, :, P * c:P * (c + 1)].rearrange("p t (q j) -> p t q j", q=NQ)
                         ).then_inc(w_ready, 1)

            def transpose_item(count, tiles=DT):
                dve.wait_ge(item_loaded, count * (16 * NQ))
                transpose_blocks(a_tf, a_in, tiles).then_inc(item_t, 1)

            def split_half(count, half):
                dve.wait_ge(xt_hi, count)
                n = DT // 2 * BANK
                sl = slice(DT // 2 * half, DT // 2 * (half + 1))
                minus_hi(a_xt[:, LO, sl, :].rearrange("p t n -> p (t n)"), a_tf[:, n * half:n * (half + 1)],
                         a_xt[:, HI, sl, :].rearrange("p t n -> p (t n)")).then_inc(xt_ready, 1)

            def split_wt(e):
                dve.wait_ge(wt_hi, e + 1)
                minus_hi(a_wt[:, 16 * KW:32 * KW], a_tf, a_wt[:, 0:16 * KW]).then_inc(wt_ready, 1)

            def evacuate_q(k):
                for c in range(CT):
                    dve.wait_ge(q_hi, k * CT + c + 1)
                    minus_hi(a_q[:, :, c, LO, :], bank[c][:].rearrange("p (u n) -> p u n", u=TPB),
                             a_q[:, :, c, HI, :]).then_inc(q_ready, 1)

            transpose_item(1)
            split_half(1, 0)
            split_half(2, 1)
            for k in range(NHB - 1):
                item = HEAD.index(HEAD_BLOCKS[k + 1])
                if HEAD[item - 1][0] == "E":
                    e = int(HEAD[item - 1][1])
                    dve.wait_ge(xt_ready, 2 * (k + 1))
                    transpose_item(item, CT if e == 2 else DT)
                    split_wt(e)
                    dve.wait_ge(wt_ready, e + 1)
                else:
                    dve.wait_ge(xt_ready, 2 * (k + 1))
                transpose_item(item + 1)
                split_half(2 * k + 3, 0)
                evacuate_q(k)
                split_half(2 * k + 4, 1)
            with dve.Fori(NHB - 1, NBLOCKS - 1) as k:
                dve.wait_ge(xt_ready, k * 2 + 2)
                transpose_item(k + (item_of_x(0) - GB) + 2)
                split_half(k * 2 + 3, 0)
                evacuate_q(k)
                split_half(k * 2 + 4, 1)

            def mt_transpose(b, j):
                dve.wait_ge(mt_loaded[j], (b + 1) * (16 * NQ))
                transpose_blocks(b_tf[j % 2], b_in[j], CT).then_inc(mt_t, 1)

            def mt_split(b, j):
                dve.wait_ge(mt_hi, b * MB + j + 1)
                minus_hi(b_mt[:, j, LO].rearrange("p t m -> p (t m)"), b_tf[j % 2],
                         b_mt[:, j, HI].rearrange("p t m -> p (t m)")).then_inc(mt_ready, 1)

            def mn_split(b, j):
                dve.wait_ge(mn_hi, b * MB + j + 1)
                minus_hi(b_mn[:, j, LO].rearrange("p s c -> p (s c)"), b_in[j],
                         b_mn[:, j, HI].rearrange("p s c -> p (s c)")).then_inc(mn_ready, 1)

            def block_max(unit, j):
                dve.wait_ge(s_done, unit * MB + j + 1)
                nc.vector.reduce_max(max_part[:, j:j + 1], bank[j][:], AX_X).then_inc(max_done, 1)

            def unit_max(unit):
                dve.wait_ge(max_done, unit * MB + MB)
                nc.vector.reduce_max(row_max[:], max_part[:], AX_X).then_inc(max_all, 1)
                dve.wait_ge(max_all, unit + 1)
                nc.vector.tensor_scalar(neg_max[:], row_max[:], -SCALE, None, ALU.mult).then_inc(neg_ready, 1)

            def unit_sum(unit):
                dve.wait_ge(exp_done, unit * MB + MB)
                nc.vector.reduce_sum(row_sum[:], sum_part[:], AX_X).then_inc(sum_done, 1)

            def unit_inverse(unit):
                dve.wait_ge(sum_done, unit + 1)
                nc.vector.reciprocal(row_inv[:], row_sum[:]).then_inc(inv_done, 1)

            def normalise_am(i, stored):
                dve.wait_ge(av_done, i + 1)
                if stored:
                    dve.wait_ge(am_stored, i * 64)
                dve.wait_ge(inv_done, i + 1)
                nc.vector.tensor_scalar(am_out[:], ps_am[:], row_inv[:], None, ALU.mult).then_inc(am_ready, 1)

            def step_dve(i, mn_of=None, mt_of=None, softmax=True, stored=True):
                for g in range(MB):
                    if softmax:
                        block_max(i + 1, g)
                    dve.wait_ge(pt_hi, i * MB + g + 1)
                    minus_hi(b_pt[:, LO, TPB * g:TPB * (g + 1), :].rearrange("p k n -> p (k n)"), ps_t[g % 2][:],
                             b_pt[:, HI, TPB * g:TPB * (g + 1), :].rearrange("p k n -> p (k n)")
                             ).then_inc(pt_ready, 1)
                    if mn_of is not None:
                        mn_split(mn_of, g)
                if softmax:
                    unit_max(i + 1)
                if mt_of is not None:
                    mt_split(mt_of, 0)
                    dve.wait_ge(mt_ready, mt_of * MB + 1)
                    mt_transpose(mt_of, 2)
                    mt_split(mt_of, 1)
                    dve.wait_ge(mt_ready, mt_of * MB + 2)
                    mt_transpose(mt_of, 3)
                    mt_split(mt_of, 2)
                    mt_split(mt_of, 3)
                if softmax:
                    dve.wait_ge(inv_done, i + 1)
                    unit_sum(i + 1)
                normalise_am(i, stored)
                if softmax:
                    dve.wait_ge(am_ready, i + 1)
                    unit_inverse(i + 1)

            mt_transpose(0, 0)
            mt_transpose(0, 1)
            mt_split(0, 0)
            mt_split(0, 1)
            evacuate_q(NBLOCKS - 1)
            dve.wait_ge(mt_ready, 2)
            mt_transpose(0, 2)
            mt_transpose(0, 3)
            mt_split(0, 2)
            mt_split(0, 3)
            for j in range(MB):
                block_max(0, j)
            unit_max(0)
            unit_sum(0)
            unit_inverse(0)
            step_dve(0, mn_of=0, stored=False)
            with dve.Fori(0, NB - 1) as b:
                with dve.Fori(1, 6) as u:
                    step_dve(b * UPB + u)
                dve.wait_ge(mt_ready, b * MB + MB)
                mt_transpose(b + 1, 0)
                mt_transpose(b + 1, 1)
                step_dve(b * UPB + 6, mt_of=b + 1)
                step_dve(b * UPB + 7)
                step_dve(b * UPB + 8, mn_of=b + 1)
            LB = (NB - 1) * UPB
            with dve.Fori(1, 7) as u:
                step_dve(LB + u)
            def transpose_x(k):
                dve.wait_ge(xin_loaded, (k + 1) * (16 * NQ))
                transpose_blocks(c_xtf, c_xin, DT).then_inc(cx_t, 1)

            def transpose_am(k):
                dve.wait_ge(ain_loaded, (k + 1) * 16)
                transpose_blocks(c_atf, c_ain, CT).then_inc(ca_t, 1)

            transpose_x(0)
            transpose_am(0)
            step_dve(LB + 7, softmax=False)

            def split_x(k):
                dve.wait_ge(cx_hi, k + 1)
                minus_hi(c_xt[LO], c_xtf, c_xt[HI]).then_inc(cx_ready, 1)

            def split_am(k):
                dve.wait_ge(ca_hi, k + 1)
                minus_hi(c_at[LO], c_atf, c_at[HI]).then_inc(ca_ready, 1)

            def unit_dve(k, following=True, stored=True):
                if following:
                    dve.wait_ge(cx_ready, k + 1)
                    transpose_x(k + 1)
                    split_x(k + 1)
                for h in range(DH):
                    dve.wait_ge(z_done, k * DH + h + 1)
                    cols = slice(BANK * h, BANK * (h + 1))
                    nc.vector.tensor_tensor(c_z[:, cols], ps_z[h][:], c_bias[:, cols], ALU.add
                                            ).then_inc(z_biased, 1)
                if following:
                    dve.wait_ge(ca_ready, k + 1)
                    transpose_am(k + 1)
                for h in range(DH):
                    dve.wait_ge(gate_done, k * DH + h + 1)
                    dve.wait_ge(c_done, k * DH + h + 1)
                    if stored:
                        dve.wait_ge(out_ready, k)
                    cols = slice(BANK * h, BANK * (h + 1))
                    nc.vector.tensor_tensor(c_u[:, cols], ps_c[h][:], c_z[:, cols], ALU.mult).then_inc(mul_done, 1)
                if following:
                    split_am(k + 1)
                dve.wait_ge(mul_done, k * DH + DH)
                dve.wait_ge(xres_loaded, (k + 1) * 16)
                nc.vector.tensor_tensor(c_u, c_u, c_xres, ALU.add).then_inc(fused_done, 1)
                dve.wait_ge(sq_done, k + 1)
                nc.vector.tensor_scalar(mean_sq[:], sq_sum[:], 1.0 / D, RMS_EPS, ALU.mult, ALU.add
                                        ).then_inc(var_done, 1)
                dve.wait_ge(rstd_done, k + 1)
                if stored:
                    dve.wait_ge(out_stored, k * 16)
                nc.vector.scalar_tensor_tensor(out=c_out, in0=c_u, scalar=rstd[:], in1=c_nw, op0=ALU.mult,
                                               op1=ALU.mult).then_inc(out_ready, 1)

            dve.wait_ge(av_done, NUNIT)
            split_x(0)
            split_am(0)
            dve.wait_ge(vec_loaded, 32)
            unit_dve(0, stored=False)
            with dve.Fori(1, NUNIT - 1) as k:
                unit_dve(k)
            unit_dve(NUNIT - 1, following=False)

        @block.tensor
        def _(pe):
            def product(dst, lhs, rhs, first, last):
                for n, (a, b) in enumerate(PASSES):
                    mm = nc.tensor.matmul(dst, lhs(a), rhs(b), start=first and n == 0,
                                          stop=last and n == len(PASSES) - 1)
                return mm

            def block_q(k, bank_free):
                for half in range(2):
                    pe.wait_ge(xt_ready, k * 2 + half + 1)
                    for c in range(CT):
                        if half == 0 and bank_free:
                            pe.wait_ge(q_ready, (k - 1) * CT + c + 1)
                        tiles = range(DT // 2 * half, DT // 2 * (half + 1))
                        for t in tiles:
                            mm = product(bank[c][:], lambda a: a_w[:, a, t, P * c:P * (c + 1)],
                                         lambda b: a_xt[:, b, t, :], t == 0, t == DT - 1)
                        if half == 1:
                            mm.then_inc(q_done, 1)
                    if half == 0:
                        mm.then_inc(q_half, 1)

            pe.wait_ge(w_ready, CT)
            block_q(0, False)
            with pe.Fori(1, NBLOCKS) as k:
                block_q(k, True)

            def scores(unit, j):
                for t in range(CT):
                    mm = product(bank[j][:], lambda a: b_q[:, t, a, :], lambda b: b_mt[:, j, b, t, :],
                                 t == 0, t == CT - 1)
                mm.then_inc(s_done, 1)

            def step_pe(i, next_mt=None, own_mn=None, softmax=True, am_before=True):
                if softmax:
                    pe.wait_ge(uq_loaded, (i + 2) * 16)
                for g in range(MB):
                    if softmax:
                        pe.wait_ge(exp_done, i * MB + g + 1)
                        if next_mt is not None:
                            pe.wait_ge(mt_ready, next_mt * MB + g + 1)
                        scores(i + 1, g)
                    else:
                        pe.wait_ge(exp_done, i * MB + g + 1)
                    if g >= 2:
                        pe.wait_ge(pt_ready, i * MB + g - 1)
                    for s in range(TPB):
                        m = TPB * g + s
                        tr = nc.tensor.transpose(ps_t[g % 2][:, P * s:P * (s + 1)], prob[:, P * m:P * (m + 1)],
                                                 ident[:])
                    tr.then_inc(t_done, 1)
                if am_before:
                    pe.wait_ge(am_ready, i)
                for g in range(MB):
                    pe.wait_ge(pt_ready, i * MB + g + 1)
                    if own_mn is not None:
                        pe.wait_ge(mn_ready, own_mn * MB + g + 1)
                    for s in range(TPB):
                        m = TPB * g + s
                        mm = product(ps_am[:], lambda a: b_pt[:, a, m, :], lambda b: b_mn[:, g, b, s, :],
                                     m == 0, m == MB * TPB - 1)
                mm.then_inc(av_done, 1)

            pe.wait_ge(const_ready, 1)
            pe.wait_ge(uq_loaded, 16)
            for j in range(MB):
                pe.wait_ge(q_ready, CT * (NBLOCKS - 1) + j + 1)
                pe.wait_ge(mt_ready, j + 1)
                scores(0, j)
            step_pe(0, own_mn=0, am_before=False)

            with pe.Fori(0, NB - 1) as b:
                with pe.Fori(1, 7) as u:
                    step_pe(b * UPB + u)
                step_pe(b * UPB + 7, next_mt=b + 1)
                step_pe(b * UPB + 8, own_mn=b + 1)
            LB = (NB - 1) * UPB
            with pe.Fori(1, 7) as u:
                step_pe(LB + u)
            step_pe(LB + 7, softmax=False)

            def x_tile(a, t):
                return c_xt[a][:, P * t:P * (t + 1)]

            def am_tile(a, t):
                return c_at[a][:, P * t:P * (t + 1)]

            def unit_c(k, first=False):
                pe.wait_ge(cx_ready, k + 1)
                if not first:
                    pe.wait_ge(z_biased, k * DH)
                for t in range(DT):
                    if first:
                        pe.wait_ge(wg1_loaded[t], 16)
                    for h in range(DH):
                        mm = product(ps_z[h][:], lambda a: x_tile(a, t),
                                     lambda b: c_wg1[:, t, b, BANK * h:BANK * (h + 1)], t == 0, False)
                mm.then_inc(cx_used, 1)
                pe.wait_ge(ca_ready, k + 1)
                if first:
                    pe.wait_ge(wc_loaded, 16 * CT)
                for h in range(DH):
                    for t in range(CT):
                        mm = product(ps_z[h][:], lambda a: am_tile(a, t),
                                     lambda b: c_wc[:, t, b, BANK * h:BANK * (h + 1)], False, t == CT - 1)
                    mm.then_inc(z_done, 1)
                if first:
                    pe.wait_ge(wm_loaded, 16 * CT)
                else:
                    pe.wait_ge(mul_done, k * DH)
                for h in range(DH):
                    for t in range(CT):
                        mm = product(ps_c[h][:], lambda a: am_tile(a, t),
                                     lambda b: c_wm[:, t, b, BANK * h:BANK * (h + 1)], t == 0, t == CT - 1)
                    mm.then_inc(c_done, 1)

            unit_c(0, first=True)
            with pe.Fori(1, NUNIT) as k:
                unit_c(k)


_INS = ["x", "ctx_1024", "L0_xattn_W_mem", "L0_xattn_W_gate", "L0_xattn_b_gate", "L0_xattn_norm_w"]


def kernel(**inputs):
    import numpy as _np
    import concourse.bacc as _bacc
    from concourse import mybir as _mybir
    from concourse.bass_utils import run_bass_kernel_spmd as _run

    nc = _bacc.Bacc("TRN2", target_bir_lowering=False, num_devices=1)
    arrays, args = {}, []
    for name in _INS:
        a = _np.ascontiguousarray(inputs[name])
        arrays[f"in_{name}"] = a
        args.append(nc.dram_tensor(f"in_{name}", a.shape, _mybir.dt.from_np(a.dtype), kind="ExternalInput").ap())
    shape = inputs["x"].shape
    out = nc.dram_tensor("out", shape, _mybir.dt.float32, kind="ExternalOutput").ap()
    build(nc, *args, out)
    r = _run(nc, [arrays], core_ids=[0])
    return r.results[0]["out"]
```

```python
from contextlib import ExitStack

import concourse.bass as bass
from concourse import mybir

ALU = mybir.AluOpType
ACT = mybir.ActivationFunctionType
AX_X = mybir.AxisListType.X
F32 = mybir.dt.float32
F32R = mybir.dt.float32r

P = 128
NQ = 4
SQ = 32
BANK = 512
HI, LO = 0, 1
PASSES = ((HI, HI), (HI, LO), (LO, HI))
RMS_EPS = 1e-6


def build(nc, x, mem, w_mem, w_gate, b_gate, norm_w, out):
    NB, N, D = x.shape
    _, M, C = mem.shape
    ROWS = NB * N
    NBLK = ROWS // BANK
    NUNIT = ROWS // P
    UPB = N // P
    DT = D // P
    CT = C // P
    MB = M // BANK
    TPB = BANK // P
    DH = D // BANK
    GB = D // BANK
    CHX = D // NQ
    CHC = C // NQ
    SCALE = float(D) ** -0.5
    assert C == BANK and M % BANK == 0 and MB == 4 and DT == 8 and UPB == 8 and DH == 2

    x_rows = x.rearrange("b n d -> (b n) d")
    out_rows = out.rearrange("b n d -> (b n) d")

    q_dram = nc.dram_tensor("q_scratch", [NUNIT, P, CT * 2 * P], F32).ap()
    am_dram = nc.dram_tensor("am_scratch", [NUNIT, P, TPB * CHC], F32).ap()
    prob_dram = nc.dram_tensor("prob_scratch", [NUNIT, P, M], F32).ap()
    wg1_dram = nc.dram_tensor("wg1_scratch", [P, DT, 2, D], F32).ap()
    wm_dram = nc.dram_tensor("wm_scratch", [P, CT, 2, D], F32).ap()
    wc_dram = nc.dram_tensor("wc_scratch", [P, CT, 2, D], F32).ap()

    with ExitStack() as ctx:
        def sb(name, shape, dt):
            return ctx.enter_context(nc.sbuf_tensor(name, shape, dt))

        def sem(name):
            return ctx.enter_context(nc.semaphore(name))

        KW = 256
        R1 = sb("region_t", [P, 64 * KW], F32R)
        R2 = sb("region_n", [P, 64 * KW], F32R)
        R3 = sb("region_l", [P, 20 * KW], F32R)
        F = sb("region_f", [P, 48 * KW], F32)
        prob = sb("prob", [P, M], F32)
        am_out = sb("am_out", [P, C], F32)
        max_part = sb("max_part", [P, MB], F32)
        row_max = sb("row_max", [P, 1], F32)
        neg_max = sb("neg_max", [P, 1], F32)
        sum_part = sb("sum_part", [P, MB], F32)
        row_sum = sb("row_sum", [P, 1], F32)
        row_inv = sb("row_inv", [P, 1], F32)
        sq_sum = sb("sq_sum", [P, 1], F32)
        mean_sq = sb("mean_sq", [P, 1], F32)
        rstd = sb("rstd", [P, 1], F32)
        m_half = sb("minus_half", [P, 1], F32)

        a_wt = R1[:, 0:32 * KW]
        a_xt = R1[:, 32 * KW:64 * KW].rearrange("p (h t n) -> p h t n", h=2, t=DT)
        a_w = R2[:, 0:32 * KW].rearrange("p (h t c) -> p h t c", h=2, t=DT)
        a_q = R2[:, 32 * KW:48 * KW].rearrange("p (u c h n) -> p u c h n", u=TPB, c=CT, h=2)
        a_in = F[:, 0:16 * KW]
        a_tf = F[:, 16 * KW:32 * KW]
        a_wf = F[:, 32 * KW:48 * KW].rearrange("p (t c) -> p t c", t=DT)
        a_ef = F[:, 32 * KW:48 * KW]
        b_mt = R1[:, :].rearrange("p (j h t m) -> p j h t m", j=MB, h=2, t=CT)
        b_mn = R2[:, :].rearrange("p (j h s c) -> p j h s c", j=MB, h=2, s=TPB)
        b_pt = R3[:, 0:16 * KW].rearrange("p (h k n) -> p h k n", h=2, k=MB * TPB)
        b_q = R3[:, 16 * KW:20 * KW].rearrange("p (c h n) -> p c h n", c=CT, h=2)
        b_in = [F[:, 8 * KW * s:8 * KW * (s + 1)] for s in range(4)]
        b_tf = [F[:, 4 * KW * s:4 * KW * (s + 1)] for s in (8, 9)]
        b_px = F[:, 40 * KW:48 * KW]
        c_wg1 = R1[:, :].rearrange("p (t h d) -> p t h d", t=DT, h=2)
        c_wc = R2[:, 0:32 * KW].rearrange("p (t h d) -> p t h d", t=CT, h=2)
        c_wm = R2[:, 32 * KW:64 * KW].rearrange("p (t h d) -> p t h d", t=CT, h=2)
        c_xt = [R3[:, 16 * KW:20 * KW], R3[:, 0:4 * KW]]
        c_at = [R3[:, 4 * KW:6 * KW], R3[:, 6 * KW:8 * KW]]
        c_xin, c_xtf, c_xres, c_z, c_u, c_out, c_bias, c_nw = (
            F[:, 4 * KW * s:4 * KW * (s + 1)] for s in range(8))
        c_ain, c_atf = (F[:, 32 * KW + 2 * KW * s:32 * KW + 2 * KW * (s + 1)] for s in range(2))
        c_sq = F[:, 36 * KW:40 * KW]

        bank = [ctx.enter_context(nc.psum_tensor(f"bank{i}", [P, BANK], F32)) for i in range(7)]
        ps_t = bank[4:6]
        ps_am = bank[6]
        ps_z, ps_c = bank[0:2], bank[2:4]

        const_ready = sem("const_ready")
        w_loaded, g0_loaded = [sem(f"w_loaded{h}") for h in range(2)], [sem(f"g0_loaded{h}") for h in range(2)]
        w_hi, w_ready, g0_half_t = sem("w_hi"), sem("w_ready"), sem("g0_half_t")
        item_loaded, item_t = sem("item_loaded"), sem("item_t")
        xt_hi, xt_ready = sem("xt_hi"), sem("xt_ready")
        wt_hi, wt_ready, wt_stored = sem("wt_hi"), sem("wt_ready"), sem("wt_stored")
        q_half, q_done = sem("q_half"), sem("q_done")
        q_hi, q_ready = sem("q_hi"), sem("q_ready")
        wc_stored, q_stored = sem("wc_stored"), sem("q_stored")
        mt_loaded = [sem(f"mt_loaded{j}") for j in range(MB)]
        mn_loaded = [sem(f"mn_loaded{j}") for j in range(MB)]
        mt_t, mt_hi, mt_ready = sem("mt_t"), sem("mt_hi"), sem("mt_ready")
        mn_hi, mn_ready = sem("mn_hi"), sem("mn_ready")
        uq_loaded = sem("uq_loaded")
        s_done, max_done, max_all, neg_ready = sem("s_done"), sem("max_done"), sem("max_all"), sem("neg_ready")
        exp_done, sum_done, inv_done = sem("exp_done"), sem("sum_done"), sem("inv_done")
        p_stored = [sem(f"p_stored{j}") for j in range(MB)]
        px_loaded = sem("px_loaded")
        pt_t, pt_hi, pt_ready = sem("pt_t"), sem("pt_hi"), sem("pt_ready")
        av_done, am_ready, am_stored = sem("av_done"), sem("am_ready"), sem("am_stored")
        wg1_loaded = [sem(f"wg1_loaded{t}") for t in range(DT)]
        wc_loaded, wm_loaded, vec_loaded = sem("wc_loaded"), sem("wm_loaded"), sem("vec_loaded")
        xin_loaded, ain_loaded, xres_loaded = sem("xin_loaded"), sem("ain_loaded"), sem("xres_loaded")
        cx_t, cx_hi, cx_ready, cx_used = sem("cx_t"), sem("cx_hi"), sem("cx_ready"), sem("cx_used")
        ca_t, ca_hi, ca_ready = sem("ca_t"), sem("ca_hi"), sem("ca_ready")
        z_done, z_biased, gate_done = sem("z_done"), sem("z_biased"), sem("gate_done")
        c_done, mul_done, fused_done = sem("c_done"), sem("mul_done"), sem("fused_done")
        sq_done, var_done, rstd_done = sem("sq_done"), sem("var_done"), sem("rstd_done")
        out_ready, out_stored = sem("out_ready"), sem("out_stored")

        HEAD = ("G0", "G1", "E0", "X0", "X1", "E1", "X2", "X3", "E2", "X4")
        HEAD_BLOCKS = tuple(name for name in HEAD if name[0] != "E")
        NHB = len(HEAD_BLOCKS)
        NHX = NHB - GB
        NBLOCKS = GB + NBLK

        def item_of_x(n):
            return n + len(HEAD) - NHX

        def load_quadrants(eng, dst, src, width, signal, part=(0, 1)):
            chunk = width // NQ
            lo, hi = chunk // part[1] * part[0], chunk // part[1] * (part[0] + 1)
            v = dst.rearrange("p (b f) -> p b f", f=chunk)
            for q in range(NQ):
                eng.dma_start(v[SQ * q:SQ * (q + 1), :, lo:hi],
                              src[:, chunk * q + lo:chunk * q + hi].rearrange("(b i) f -> i b f", i=SQ)
                              ).then_inc(signal, 16)

        def transpose_blocks(dst, src, tiles, part=(0, 1)):
            ts = slice(tiles // part[1] * part[0], tiles // part[1] * (part[0] + 1))
            return nc.vector.transpose(dst.rearrange("p (t b i) -> p t b i", t=tiles, i=SQ)[:, ts],
                                       src.rearrange("p (b t j) -> p t b j", t=tiles, j=SQ)[:, ts])

        def w_quarter(half, c):
            ts = slice(DT // 2 * half, DT // 2 * (half + 1))
            return (a_wf.rearrange("p t (q c j) -> p t c q j", q=NQ, j=SQ)[:, ts, c],
                    *(a_w[:, part, ts, P * c:P * (c + 1)].rearrange("p t (q j) -> p t q j", q=NQ)
                      for part in (HI, LO)))

        HPJ = 2
        MTS = MB * HPJ

        def mt_half(part, h):
            w = BANK // HPJ
            return b_mt[:, h // HPJ, part, :, w * (h % HPJ):w * (h % HPJ + 1)]

        def tf_half(h):
            return b_tf[h % 2].rearrange("p (t m) -> p t m", t=CT)

        def minus_hi(dst, src, hi):
            return nc.vector.tensor_tensor(dst, src, hi.bitcast(F32), ALU.subtract)

        block = ctx.enter_context(nc.Block())

        @block.sync
        def _(sp):
            for h in range(2):
                for q in range(NQ):
                    sp.dma_start(a_wf[SQ * q:SQ * (q + 1), DT // 2 * h:DT // 2 * (h + 1)],
                                 w_mem[CHX * q + CHX // 2 * h:CHX * q + CHX // 2 * (h + 1), :].rearrange(
                                     "(t j) c -> j t c", j=SQ)).then_inc(w_loaded[h], 16)
                load_quadrants(sp, a_in, w_gate[0:BANK, D:2 * D], D, g0_loaded[h], part=(h, 2))

            def load_item(name, n):
                sp.wait_ge(item_t, n)
                k = int(name[1])
                if name[0] == "G":
                    load_quadrants(sp, a_in, w_gate[BANK * k:BANK * (k + 1), D:2 * D], D, item_loaded)
                elif name[0] == "X":
                    load_quadrants(sp, a_in, x_rows[BANK * k:BANK * (k + 1), :], D, item_loaded)
                elif name == "E2":
                    load_quadrants(sp, a_in, w_mem, C, item_loaded)
                else:
                    load_quadrants(sp, a_in, w_gate[BANK * k:BANK * (k + 1), 0:D], D, item_loaded)

            def store_wt(e):
                sp.wait_ge(wt_ready, e + 1)
                if e < 2:
                    v = a_wt.bitcast(F32).rearrange("p (h t n) -> p t h n", h=2, t=DT)
                    for h in range(2):
                        sp.dma_start(wg1_dram[:, :, h, BANK * e:BANK * (e + 1)], v[:, :, h]).then_inc(wt_stored, 16)
                else:
                    v = a_wt.bitcast(F32).rearrange("p (h t n) -> p t h n", h=2, t=CT)
                    for h in range(2):
                        sp.dma_start(wm_dram[:, :, h, :], v[:, :, h]).then_inc(wt_stored, 16)

            def store_wc(k):
                sp.wait_ge(q_ready, CT * (k + 1))
                for u in range(TPB):
                    sp.dma_start(wc_dram[:, :, :, BANK * k + P * u:BANK * k + P * (u + 1)],
                                 a_q[:, u].bitcast(F32)).then_inc(wc_stored, 16)

            def store_q(n):
                sp.wait_ge(q_ready, (n + (GB + 1)) * CT)
                sp.dma_start(q_dram[bass.ds(n * TPB, TPB)].rearrange("u p f -> p u f"),
                             a_q.bitcast(F32).rearrange("p u c h n -> p u (c h n)")).then_inc(q_stored, 16)

            load_item("G1", 1)
            load_item("E0", 2)
            load_item("X0", 3)
            store_wc(0)
            store_wt(0)
            load_item("X1", 4)
            store_wc(1)
            load_item("E1", 5)
            load_item("X2", 6)
            store_q(0)
            store_wt(1)
            load_item("X3", 7)
            store_q(1)
            load_item("E2", 8)
            load_item("X4", 9)
            store_q(2)
            store_wt(2)
            with sp.Fori(NHX, NBLK) as n:
                sp.wait_ge(item_t, n + item_of_x(0))
                load_quadrants(sp, a_in, x_rows[bass.ds(n * BANK, BANK), :], D, item_loaded)
                store_q(n - 2)

            def load_mt(b, j):
                load_quadrants(sp, b_in[j], mem[b, BANK * j:BANK * (j + 1), :], C, mt_loaded[j])

            def load_mn(b, j):
                v = b_in[j].rearrange("p (s c) -> p s c", s=TPB)
                for q in range(NQ):
                    r = M // NQ * q + P * j
                    sp.dma_start(v[SQ * q:SQ * (q + 1)],
                                 mem[b, r:r + P, :].rearrange("(s i) c -> i s c", i=SQ)).then_inc(mn_loaded[j], 16)

            def load_q(unit):
                sp.dma_start(b_q.bitcast(F32).rearrange("p c h n -> p (c h n)"), q_dram[unit]).then_inc(uq_loaded, 16)

            def store_am(i):
                sp.wait_ge(am_ready, i + 1)
                v = am_dram[i].rearrange("(q i) (b c) -> b i q c", q=NQ, b=TPB)
                for b in range(TPB):
                    sp.dma_start(v[b], am_out[SQ * b:SQ * (b + 1), :].rearrange("i (q c) -> i q c", q=NQ)
                                 ).then_inc(am_stored, 16)

            sp.wait_ge(item_t, item_of_x(NBLK))
            load_mt(0, 0)
            load_mt(0, 1)
            store_q(NBLK - 2)
            sp.wait_ge(xt_ready, 2 * NBLOCKS)
            load_mt(0, 2)
            load_mt(0, 3)
            sp.wait_ge(q_stored, 16 * (NBLK - 1))
            load_q(0)
            sp.wait_ge(mt_t, 2 * HPJ)
            load_mn(0, 0)
            load_mn(0, 1)
            store_q(NBLK - 1)

            def exchange(unit, first=False):
                def there(j):
                    sp.wait_ge(exp_done, unit * MB + j + 1)
                    cols = slice(BANK * j, BANK * (j + 1))
                    sp.dma_start(prob_dram[unit, :, cols], prob[:, cols]).then_inc(p_stored[j], 16)

                def back(j):
                    sp.wait_ge(p_stored[j], (unit + 1) * 16)
                    if j == 0 and not first:
                        sp.wait_ge(pt_t, unit * MB)
                    sp.dma_start(b_px[SQ * j:SQ * (j + 1)].rearrange("i (b m) -> i b m", b=TPB),
                                 prob_dram[unit, :, BANK * j:BANK * (j + 1)].rearrange("(b i) m -> i b m", i=SQ)
                                 ).then_inc(px_loaded, 16)

                there(0)
                there(1)
                for j in range(2, MB):
                    there(j)
                    back(j - 2)
                back(MB - 2)
                back(MB - 1)

            sp.wait_ge(mt_t, MTS)
            load_mn(0, 2)
            load_mn(0, 3)
            sp.wait_ge(s_done, MB)
            load_q(1)
            exchange(0, first=True)

            def step_sp(i, unit_after_next=True, softmax=True):
                if unit_after_next:
                    sp.wait_ge(s_done, (i + 2) * MB)
                    load_q(i + 2)
                if softmax:
                    exchange(i + 1)
                store_am(i)

            def load_next_mt(b):
                sp.wait_ge(mn_ready, (b + 1) * MB)
                for j in range(MB):
                    load_mt(b + 1, j)

            def load_next_mn(b, j):
                sp.wait_ge(mt_t, (b + 1) * MTS + HPJ * (j + 1))
                load_mn(b + 1, j)

            sp.wait_ge(q_stored, 16 * NBLK)
            step_sp(0)
            with sp.Fori(0, NB - 1) as b:
                load_next_mt(b)
                with sp.Fori(1, 6) as u:
                    step_sp(b * UPB + u)
                load_next_mn(b, 0)
                sp.wait_ge(s_done, (b * UPB + 8) * MB)
                load_q(b * UPB + 8)
                exchange(b * UPB + 7)
                for j in range(1, MB):
                    load_next_mn(b, j)
                store_am(b * UPB + 6)
                step_sp(b * UPB + 7)
                step_sp(b * UPB + 8)
            LB = (NB - 1) * UPB

            sp.wait_ge(mn_ready, NB * MB)
            sp.dma_start(c_bias, b_gate.rearrange("(a d) -> a d", a=1).to_broadcast([P, D])).then_inc(vec_loaded, 16)
            sp.dma_start(c_nw, norm_w.rearrange("(a d) -> a d", a=1).to_broadcast([P, D])).then_inc(vec_loaded, 16)
            sp.dma_start(c_xres, x_rows[0:P, :]).then_inc(xres_loaded, 16)
            load_quadrants(sp, c_xin, x_rows[0:P, :], D, xin_loaded)
            sp.wait_ge(am_stored, 64)
            sp.dma_start(c_ain, am_dram[0]).then_inc(ain_loaded, 16)
            with sp.Fori(1, 6) as u:
                step_sp(LB + u)
            exchange(NUNIT - 1)
            sp.wait_ge(s_done, NUNIT * MB)
            sp.wait_ge(wt_stored, 3 * 32)
            for t in range(DT):
                sp.dma_start(c_wg1[:, t].bitcast(F32), wg1_dram[:, t]).then_inc(wg1_loaded[t], 16)
            store_am(NUNIT - 2)
            sp.wait_ge(av_done, NUNIT)
            sp.wait_ge(wc_stored, 2 * 64)
            for t in range(CT):
                sp.dma_start(c_wc[:, t].bitcast(F32), wc_dram[:, t]).then_inc(wc_loaded, 16)
            for t in range(CT):
                sp.dma_start(c_wm[:, t].bitcast(F32), wm_dram[:, t]).then_inc(wm_loaded, 16)
            store_am(NUNIT - 1)
            sp.wait_ge(am_stored, 64 * NUNIT)

            def load_inputs(k):
                sp.wait_ge(cx_t, k)
                load_quadrants(sp, c_xin, x_rows[bass.ds(k * P, P), :], D, xin_loaded)
                sp.wait_ge(ca_t, k)
                sp.dma_start(c_ain, am_dram[k]).then_inc(ain_loaded, 16)

            def store_out(k):
                sp.wait_ge(out_ready, k + 1)
                sp.dma_start(out_rows[bass.ds(k * P, P), :], c_out).then_inc(out_stored, 16)

            def next_residual(k):
                sp.wait_ge(fused_done, k + 1)
                sp.dma_start(c_xres, x_rows[bass.ds(k * P + P, P), :]).then_inc(xres_loaded, 16)

            load_inputs(1)
            with sp.Fori(0, NUNIT - 2) as k:
                load_inputs(k + 2)
                next_residual(k)
                store_out(k)
            next_residual(NUNIT - 2)
            store_out(NUNIT - 2)
            store_out(NUNIT - 1)
            sp.wait_ge(out_stored, 16 * NUNIT)

        @block.gpsimd
        def _(pool):
            nc.gpsimd.memset(m_half[:], -0.5).then_inc(const_ready, 1)
            pool.wait_ge(const_ready, 1)
            with pool.Fori(0, NUNIT) as k:
                pool.wait_ge(var_done, k + 1)
                nc.gpsimd.tensor_tensor(rstd[:], mean_sq[:], m_half[:], ALU.pow).then_inc(rstd_done, 1)

        @block.scalar
        def _(act):
            def split_w(half):
                act.wait_ge(w_loaded[half], 16 * NQ)
                for c in range(CT):
                    src, hi, _ = w_quarter(half, c)
                    nc.scalar.copy(hi, src).then_inc(w_hi, 1)

            def split_half(half):
                n = DT // 2 * BANK
                nc.scalar.copy(a_xt[:, HI, DT // 2 * half:DT // 2 * (half + 1), :].rearrange("p t n -> p (t n)"),
                               a_tf[:, n * half:n * (half + 1)]).then_inc(xt_hi, 1)

            def split_wt(e, item):
                act.wait_ge(item_t, item + 1)
                if e > 0:
                    act.wait_ge(wt_stored, 32 * e)
                nc.scalar.copy(a_wt[:, 0:16 * KW], a_ef).then_inc(wt_hi, 1)

            def evacuate_q(k, free):
                free()
                for c in range(CT):
                    act.wait_ge(q_done, k * CT + c + 1)
                    nc.scalar.copy(a_q[:, :, c, HI, :], bank[c][:].rearrange("p (u n) -> p u n", u=TPB)
                                   ).then_inc(q_hi, 1)

            split_w(0)
            act.wait_ge(g0_half_t, 1)
            split_half(0)
            split_w(1)
            act.wait_ge(item_t, 1)
            split_half(1)
            for k in range(NHB - 1):
                item = HEAD.index(HEAD_BLOCKS[k + 1])
                if HEAD[item - 1][0] == "E":
                    split_wt(int(HEAD[item - 1][1]), item - 1)
                act.wait_ge(item_t, item + 1)
                act.wait_ge(q_half, k + 1)
                split_half(0)
                if k == 0:
                    evacuate_q(k, lambda: None)
                elif k <= GB:
                    evacuate_q(k, lambda: act.wait_ge(wc_stored, 64 * k))
                else:
                    evacuate_q(k, lambda: act.wait_ge(q_stored, 16 * (k - GB)))
                split_half(1)
            with act.Fori(NHB - 1, NBLOCKS - 1) as k:
                act.wait_ge(item_t, k + (item_of_x(0) - GB) + 2)
                act.wait_ge(q_half, k + 1)
                split_half(0)
                evacuate_q(k, lambda: act.wait_ge(q_stored, (k - GB) * 16))
                split_half(1)

            def mt_split(b, halves):
                for h in halves:
                    act.wait_ge(mt_t, b * MTS + h + 1)
                    nc.scalar.copy(mt_half(HI, h), tf_half(h)).then_inc(mt_hi, 1)

            def mn_split(b, j):
                act.wait_ge(mn_loaded[j], (b + 1) * (16 * NQ))
                nc.scalar.copy(b_mn[:, j, HI].rearrange("p s c -> p (s c)"), b_in[j]).then_inc(mn_hi, 1)

            def exps(unit, stored=True):
                act.wait_ge(neg_ready, unit + 1)
                if stored:
                    for j in range(MB):
                        act.wait_ge(p_stored[j], unit * 16)
                for j in range(MB):
                    nc.scalar.activation(prob[:, BANK * j:BANK * (j + 1)], bank[j][:], ACT.Exp, bias=neg_max[:],
                                         scale=SCALE, accum_out=sum_part[:, j:j + 1]).then_inc(exp_done, 1)

            def step_act(i, mn_of=None, mt_of=None, softmax=True, first=False):
                if mn_of is not None:
                    if first:
                        act.wait_ge(q_done, NBLOCKS * CT)
                    else:
                        act.wait_ge(av_done, mn_of * UPB)
                for g in range(MB):
                    if mn_of is not None:
                        mn_split(mn_of, g)
                    act.wait_ge(pt_t, i * MB + g + 1)
                    nc.scalar.copy(b_pt[:, HI, TPB * g:TPB * (g + 1), :].rearrange("p k n -> p (k n)"),
                                   ps_t[g % 2][:]).then_inc(pt_hi, 1)
                if mt_of is not None:
                    act.wait_ge(s_done, (mt_of * UPB) * MB)
                    mt_split(mt_of, range(0, MTS // 2))
                if softmax:
                    act.wait_ge(sum_done, i + 1)
                    exps(i + 1)
                if mt_of is not None:
                    mt_split(mt_of, range(MTS // 2, MTS))

            act.wait_ge(wt_stored, 32 * 3)
            mt_split(0, range(0, MTS // 2))
            evacuate_q(NBLOCKS - 1, lambda: act.wait_ge(q_stored, 16 * (NBLK - 1)))
            mt_split(0, range(MTS // 2, MTS))
            exps(0, stored=False)
            act.wait_ge(q_stored, 16 * NBLK)
            step_act(0, mn_of=0, first=True)
            with act.Fori(0, NB - 1) as b:
                with act.Fori(1, 6) as u:
                    step_act(b * UPB + u)
                step_act(b * UPB + 6, mt_of=b + 1)
                step_act(b * UPB + 7)
                step_act(b * UPB + 8, mn_of=b + 1)
            LB = (NB - 1) * UPB
            with act.Fori(1, 7) as u:
                step_act(LB + u)
            step_act(LB + 7, softmax=False)

            def split_x(k):
                act.wait_ge(cx_t, k + 1)
                nc.scalar.copy(c_xt[HI], c_xtf).then_inc(cx_hi, 1)

            def split_am(k):
                act.wait_ge(ca_t, k + 1)
                nc.scalar.copy(c_at[HI], c_atf).then_inc(ca_hi, 1)

            def unit_act(k, following=True):
                if following:
                    act.wait_ge(cx_used, k + 1)
                    split_x(k + 1)
                for h in range(DH):
                    act.wait_ge(z_biased, k * DH + h + 1)
                    v = c_z[:, BANK * h:BANK * (h + 1)]
                    nc.scalar.activation(v, v, ACT.Sigmoid).then_inc(gate_done, 1)
                if following:
                    act.wait_ge(c_done, k * DH + DH)
                    split_am(k + 1)
                act.wait_ge(fused_done, k + 1)
                nc.scalar.activation(c_sq, c_u, ACT.Square, accum_out=sq_sum[:]).then_inc(sq_done, 1)

            split_x(0)
            act.wait_ge(av_done, NUNIT)
            split_am(0)
            with act.Fori(0, NUNIT - 1) as k:
                unit_act(k)
            unit_act(NUNIT - 1, following=False)

        @block.vector
        def _(dve):
            def split_w(half):
                for c in range(CT):
                    dve.wait_ge(w_hi, half * CT + c + 1)
                    src, hi, lo = w_quarter(half, c)
                    minus_hi(lo, src, hi).then_inc(w_ready, 1)

            def transpose_item(count, dst=a_tf, tiles=DT):
                dve.wait_ge(item_loaded, (count - 1) * (16 * NQ))
                transpose_blocks(dst, a_in, tiles).then_inc(item_t, 1)

            def split_half(count, half):
                dve.wait_ge(xt_hi, count)
                n = DT // 2 * BANK
                sl = slice(DT // 2 * half, DT // 2 * (half + 1))
                minus_hi(a_xt[:, LO, sl, :].rearrange("p t n -> p (t n)"), a_tf[:, n * half:n * (half + 1)],
                         a_xt[:, HI, sl, :].rearrange("p t n -> p (t n)")).then_inc(xt_ready, 1)

            def split_wt(e):
                dve.wait_ge(wt_hi, e + 1)
                minus_hi(a_wt[:, 16 * KW:32 * KW], a_ef, a_wt[:, 0:16 * KW]).then_inc(wt_ready, 1)

            def evacuate_q(k):
                for c in range(CT):
                    dve.wait_ge(q_hi, k * CT + c + 1)
                    minus_hi(a_q[:, :, c, LO, :], bank[c][:].rearrange("p (u n) -> p u n", u=TPB),
                             a_q[:, :, c, HI, :]).then_inc(q_ready, 1)

            for half, signal in ((0, g0_half_t), (1, item_t)):
                dve.wait_ge(g0_loaded[half], 16 * NQ)
                transpose_blocks(a_tf, a_in, DT, part=(half, 2)).then_inc(signal, 1)
                split_w(half)
                split_half(half + 1, half)
            for k in range(NHB - 1):
                item = HEAD.index(HEAD_BLOCKS[k + 1])
                if HEAD[item - 1][0] == "E":
                    split_wt(int(HEAD[item - 1][1]))
                dve.wait_ge(xt_ready, 2 * (k + 1))
                transpose_item(item + 1)
                split_half(2 * k + 3, 0)
                if item + 1 < len(HEAD) and HEAD[item + 1][0] == "E":
                    e = int(HEAD[item + 1][1])
                    if e > 0:
                        dve.wait_ge(wt_ready, e)
                    else:
                        dve.wait_ge(w_ready, 2 * CT)
                    transpose_item(item + 2, a_ef, CT if e == 2 else DT)
                evacuate_q(k)
                split_half(2 * k + 4, 1)
            with dve.Fori(NHB - 1, NBLOCKS - 1) as k:
                dve.wait_ge(xt_ready, k * 2 + 2)
                transpose_item(k + (item_of_x(0) - GB) + 2)
                split_half(k * 2 + 3, 0)
                evacuate_q(k)
                split_half(k * 2 + 4, 1)

            def mt_transpose(b, h):
                dve.wait_ge(mt_loaded[h // HPJ], (b + 1) * (16 * NQ))
                rows = b_in[h // HPJ].rearrange("p (b t j) -> p t b j", t=CT, j=SQ)
                nb = BANK // SQ // HPJ
                nc.vector.transpose(tf_half(h).rearrange("p t (b i) -> p t b i", i=SQ),
                                    rows[:, :, nb * (h % HPJ):nb * (h % HPJ + 1)]).then_inc(mt_t, 1)

            def mt_split(b, h):
                dve.wait_ge(mt_hi, b * MTS + h + 1)
                minus_hi(mt_half(LO, h), tf_half(h), mt_half(HI, h)).then_inc(mt_ready, 1)

            def mt_split_and_next(b, halves):
                for h in halves:
                    mt_split(b, h)
                    if h + 2 < MTS:
                        dve.wait_ge(mt_ready, b * MTS + h + 1)
                        mt_transpose(b, h + 2)

            def mn_split(b, j):
                dve.wait_ge(mn_hi, b * MB + j + 1)
                minus_hi(b_mn[:, j, LO].rearrange("p s c -> p (s c)"), b_in[j],
                         b_mn[:, j, HI].rearrange("p s c -> p (s c)")).then_inc(mn_ready, 1)

            def block_max(unit, j):
                dve.wait_ge(s_done, unit * MB + j + 1)
                nc.vector.reduce_max(max_part[:, j:j + 1], bank[j][:], AX_X).then_inc(max_done, 1)

            def unit_max(unit):
                dve.wait_ge(max_done, unit * MB + MB)
                nc.vector.reduce_max(row_max[:], max_part[:], AX_X).then_inc(max_all, 1)
                dve.wait_ge(max_all, unit + 1)
                nc.vector.tensor_scalar(neg_max[:], row_max[:], -SCALE, None, ALU.mult).then_inc(neg_ready, 1)

            def unit_sum(unit):
                dve.wait_ge(exp_done, unit * MB + MB)
                nc.vector.reduce_sum(row_sum[:], sum_part[:], AX_X).then_inc(sum_done, 1)

            def unit_inverse(unit):
                dve.wait_ge(sum_done, unit + 1)
                nc.vector.reciprocal(row_inv[:], row_sum[:]).then_inc(inv_done, 1)

            def normalise_am(i, stored):
                dve.wait_ge(av_done, i + 1)
                if stored:
                    dve.wait_ge(am_stored, i * 64)
                dve.wait_ge(inv_done, i + 1)
                nc.vector.tensor_scalar(am_out[:], ps_am[:], row_inv[:], None, ALU.mult).then_inc(am_ready, 1)

            def pt_transpose(i, g):
                if g >= 2:
                    dve.wait_ge(pt_ready, i * MB + g - 1)
                v = b_px.rearrange("p (b k j) -> p k b j", b=TPB, j=SQ)
                nc.vector.transpose(ps_t[g % 2][:].rearrange("p (k b i) -> p k b i", k=TPB, i=SQ),
                                    v[:, TPB * g:TPB * (g + 1)]).then_inc(pt_t, 1)

            def step_dve(i, mn_of=None, mt_of=None, softmax=True, stored=True):
                dve.wait_ge(px_loaded, (i + 1) * (16 * NQ))
                if stored:
                    dve.wait_ge(av_done, i)
                pt_transpose(i, 0)
                for g in range(MB):
                    if g + 1 < MB:
                        pt_transpose(i, g + 1)
                    if softmax:
                        block_max(i + 1, g)
                    dve.wait_ge(pt_hi, i * MB + g + 1)
                    minus_hi(b_pt[:, LO, TPB * g:TPB * (g + 1), :].rearrange("p k n -> p (k n)"), ps_t[g % 2][:],
                             b_pt[:, HI, TPB * g:TPB * (g + 1), :].rearrange("p k n -> p (k n)")
                             ).then_inc(pt_ready, 1)
                    if mn_of is not None:
                        mn_split(mn_of, g)
                if softmax:
                    unit_max(i + 1)
                if mt_of is not None:
                    mt_split_and_next(mt_of, range(MTS))
                if softmax:
                    dve.wait_ge(inv_done, i + 1)
                    unit_sum(i + 1)
                normalise_am(i, stored)
                if softmax:
                    dve.wait_ge(am_ready, i + 1)
                    unit_inverse(i + 1)

            mt_transpose(0, 0)
            mt_transpose(0, 1)
            mt_split_and_next(0, range(0, MTS // 2 - 2))
            mt_split(0, MTS // 2 - 2)
            mt_split(0, MTS // 2 - 1)
            evacuate_q(NBLOCKS - 1)
            dve.wait_ge(mt_ready, MTS // 2)
            mt_transpose(0, MTS // 2)
            mt_transpose(0, MTS // 2 + 1)
            mt_split_and_next(0, range(MTS // 2, MTS))
            for j in range(MB):
                block_max(0, j)
            unit_max(0)
            unit_sum(0)
            unit_inverse(0)
            step_dve(0, mn_of=0, stored=False)
            with dve.Fori(0, NB - 1) as b:
                with dve.Fori(1, 6) as u:
                    step_dve(b * UPB + u)
                dve.wait_ge(mt_ready, b * MTS + MTS)
                mt_transpose(b + 1, 0)
                mt_transpose(b + 1, 1)
                step_dve(b * UPB + 6, mt_of=b + 1)
                step_dve(b * UPB + 7)
                step_dve(b * UPB + 8, mn_of=b + 1)
            LB = (NB - 1) * UPB
            with dve.Fori(1, 7) as u:
                step_dve(LB + u)
            def transpose_x(k):
                dve.wait_ge(xin_loaded, (k + 1) * (16 * NQ))
                transpose_blocks(c_xtf, c_xin, DT).then_inc(cx_t, 1)

            def transpose_am(k):
                dve.wait_ge(ain_loaded, (k + 1) * 16)
                transpose_blocks(c_atf, c_ain, CT).then_inc(ca_t, 1)

            transpose_x(0)
            transpose_am(0)
            step_dve(LB + 7, softmax=False)

            def split_x(k):
                dve.wait_ge(cx_hi, k + 1)
                minus_hi(c_xt[LO], c_xtf, c_xt[HI]).then_inc(cx_ready, 1)

            def split_am(k):
                dve.wait_ge(ca_hi, k + 1)
                minus_hi(c_at[LO], c_atf, c_at[HI]).then_inc(ca_ready, 1)

            def unit_dve(k, following=True, stored=True):
                if following:
                    dve.wait_ge(cx_ready, k + 1)
                    transpose_x(k + 1)
                    split_x(k + 1)
                for h in range(DH):
                    dve.wait_ge(z_done, k * DH + h + 1)
                    cols = slice(BANK * h, BANK * (h + 1))
                    nc.vector.tensor_tensor(c_z[:, cols], ps_z[h][:], c_bias[:, cols], ALU.add
                                            ).then_inc(z_biased, 1)
                if following:
                    dve.wait_ge(ca_ready, k + 1)
                    transpose_am(k + 1)
                for h in range(DH):
                    dve.wait_ge(gate_done, k * DH + h + 1)
                    dve.wait_ge(c_done, k * DH + h + 1)
                    if stored:
                        dve.wait_ge(out_ready, k)
                    cols = slice(BANK * h, BANK * (h + 1))
                    nc.vector.tensor_tensor(c_u[:, cols], ps_c[h][:], c_z[:, cols], ALU.mult).then_inc(mul_done, 1)
                if following:
                    split_am(k + 1)
                dve.wait_ge(mul_done, k * DH + DH)
                dve.wait_ge(xres_loaded, (k + 1) * 16)
                nc.vector.tensor_tensor(c_u, c_u, c_xres, ALU.add).then_inc(fused_done, 1)
                dve.wait_ge(sq_done, k + 1)
                nc.vector.tensor_scalar(mean_sq[:], sq_sum[:], 1.0 / D, RMS_EPS, ALU.mult, ALU.add
                                        ).then_inc(var_done, 1)
                dve.wait_ge(rstd_done, k + 1)
                if stored:
                    dve.wait_ge(out_stored, k * 16)
                nc.vector.scalar_tensor_tensor(out=c_out, in0=c_u, scalar=rstd[:], in1=c_nw, op0=ALU.mult,
                                               op1=ALU.mult).then_inc(out_ready, 1)

            dve.wait_ge(av_done, NUNIT)
            split_x(0)
            split_am(0)
            dve.wait_ge(vec_loaded, 32)
            unit_dve(0, stored=False)
            with dve.Fori(1, NUNIT - 1) as k:
                unit_dve(k)
            unit_dve(NUNIT - 1, following=False)

        @block.tensor
        def _(pe):
            def product(dst, lhs, rhs, first, last):
                for n, (a, b) in enumerate(PASSES):
                    mm = nc.tensor.matmul(dst, lhs(a), rhs(b), start=first and n == 0,
                                          stop=last and n == len(PASSES) - 1)
                return mm

            def block_q(k, first=False):
                for half in range(2):
                    pe.wait_ge(xt_ready, k * 2 + half + 1)
                    for c in range(CT):
                        if half == 0 and not first:
                            pe.wait_ge(q_ready, (k - 1) * CT + c + 1)
                        if first:
                            pe.wait_ge(w_ready, CT * half + c + 1)
                        tiles = range(DT // 2 * half, DT // 2 * (half + 1))
                        for t in tiles:
                            mm = product(bank[c][:], lambda a: a_w[:, a, t, P * c:P * (c + 1)],
                                         lambda b: a_xt[:, b, t, :], t == 0, t == DT - 1)
                        if half == 1:
                            mm.then_inc(q_done, 1)
                    if half == 0:
                        mm.then_inc(q_half, 1)

            block_q(0, first=True)
            with pe.Fori(1, NBLOCKS) as k:
                block_q(k)

            def scores(unit, j):
                for t in range(CT):
                    mm = product(bank[j][:], lambda a: b_q[:, t, a, :], lambda b: b_mt[:, j, b, t, :],
                                 t == 0, t == CT - 1)
                mm.then_inc(s_done, 1)

            def step_pe(i, next_mt=None, own_mn=None, softmax=True, am_before=True):
                if softmax:
                    pe.wait_ge(uq_loaded, (i + 2) * 16)
                    for j in range(MB):
                        pe.wait_ge(exp_done, i * MB + j + 1)
                        if next_mt is not None:
                            pe.wait_ge(mt_ready, next_mt * MTS + HPJ * (j + 1))
                        scores(i + 1, j)
                if am_before:
                    pe.wait_ge(am_ready, i)
                for g in range(MB):
                    pe.wait_ge(pt_ready, i * MB + g + 1)
                    if own_mn is not None:
                        pe.wait_ge(mn_ready, own_mn * MB + g + 1)
                    for s in range(TPB):
                        m = TPB * g + s
                        mm = product(ps_am[:], lambda a: b_pt[:, a, m, :], lambda b: b_mn[:, g, b, s, :],
                                     m == 0, m == MB * TPB - 1)
                mm.then_inc(av_done, 1)

            pe.wait_ge(uq_loaded, 16)
            for j in range(MB):
                pe.wait_ge(q_ready, CT * (NBLOCKS - 1) + j + 1)
                pe.wait_ge(mt_ready, HPJ * (j + 1))
                scores(0, j)
            step_pe(0, own_mn=0, am_before=False)

            with pe.Fori(0, NB - 1) as b:
                with pe.Fori(1, 7) as u:
                    step_pe(b * UPB + u)
                step_pe(b * UPB + 7, next_mt=b + 1)
                step_pe(b * UPB + 8, own_mn=b + 1)
            LB = (NB - 1) * UPB
            with pe.Fori(1, 7) as u:
                step_pe(LB + u)
            step_pe(LB + 7, softmax=False)

            def x_tile(a, t):
                return c_xt[a][:, P * t:P * (t + 1)]

            def am_tile(a, t):
                return c_at[a][:, P * t:P * (t + 1)]

            def unit_c(k, first=False):
                pe.wait_ge(cx_ready, k + 1)
                if not first:
                    pe.wait_ge(z_biased, k * DH)
                for t in range(DT):
                    if first:
                        pe.wait_ge(wg1_loaded[t], 16)
                    for h in range(DH):
                        mm = product(ps_z[h][:], lambda a: x_tile(a, t),
                                     lambda b: c_wg1[:, t, b, BANK * h:BANK * (h + 1)], t == 0, False)
                mm.then_inc(cx_used, 1)
                pe.wait_ge(ca_ready, k + 1)
                if first:
                    pe.wait_ge(wc_loaded, 16 * CT)
                for h in range(DH):
                    for t in range(CT):
                        mm = product(ps_z[h][:], lambda a: am_tile(a, t),
                                     lambda b: c_wc[:, t, b, BANK * h:BANK * (h + 1)], False, t == CT - 1)
                    mm.then_inc(z_done, 1)
                if first:
                    pe.wait_ge(wm_loaded, 16 * CT)
                else:
                    pe.wait_ge(mul_done, k * DH)
                for h in range(DH):
                    for t in range(CT):
                        mm = product(ps_c[h][:], lambda a: am_tile(a, t),
                                     lambda b: c_wm[:, t, b, BANK * h:BANK * (h + 1)], t == 0, t == CT - 1)
                    mm.then_inc(c_done, 1)

            unit_c(0, first=True)
            with pe.Fori(1, NUNIT) as k:
                unit_c(k)


_INS = ["x", "ctx_1024", "L0_xattn_W_mem", "L0_xattn_W_gate", "L0_xattn_b_gate", "L0_xattn_norm_w"]


def kernel(**inputs):
    import numpy as _np
    import concourse.bacc as _bacc
    from concourse import mybir as _mybir
    from concourse.bass_utils import run_bass_kernel_spmd as _run

    nc = _bacc.Bacc("TRN2", target_bir_lowering=False, num_devices=1)
    arrays, args = {}, []
    for name in _INS:
        a = _np.ascontiguousarray(inputs[name])
        arrays[f"in_{name}"] = a
        args.append(nc.dram_tensor(f"in_{name}", a.shape, _mybir.dt.from_np(a.dtype), kind="ExternalInput").ap())
    shape = inputs["x"].shape
    out = nc.dram_tensor("out", shape, _mybir.dt.float32, kind="ExternalOutput").ap()
    build(nc, *args, out)
    r = _run(nc, [arrays], core_ids=[0])
    return r.results[0]["out"]
```

```python
from contextlib import ExitStack

import concourse.bass as bass
from concourse import mybir

ALU = mybir.AluOpType
ACT = mybir.ActivationFunctionType
AX_X = mybir.AxisListType.X
F32 = mybir.dt.float32
F32R = mybir.dt.float32r

P = 128
NQ = 4
SQ = 32
BANK = 512
HI, LO = 0, 1
PASSES = ((HI, HI), (HI, LO), (LO, HI))
RMS_EPS = 1e-6


def build(nc, x, mem, w_mem, w_gate, b_gate, norm_w, out):
    NB, N, D = x.shape
    _, M, C = mem.shape
    ROWS = NB * N
    NBLK = ROWS // BANK
    NUNIT = ROWS // P
    UPB = N // P
    DT = D // P
    CT = C // P
    MB = M // BANK
    TPB = BANK // P
    DH = D // BANK
    GB = D // BANK
    CHX = D // NQ
    CHC = C // NQ
    SCALE = float(D) ** -0.5
    assert C == BANK and M % BANK == 0 and MB == 4 and DT == 8 and UPB == 8 and DH == 2

    x_rows = x.rearrange("b n d -> (b n) d")
    out_rows = out.rearrange("b n d -> (b n) d")

    q_dram = nc.dram_tensor("q_scratch", [NUNIT, P, CT * 2 * P], F32).ap()
    am_dram = nc.dram_tensor("am_scratch", [NUNIT, P, TPB * CHC], F32).ap()
    prob_dram = nc.dram_tensor("prob_scratch", [NUNIT, P, M], F32).ap()
    wg1_dram = nc.dram_tensor("wg1_scratch", [P, DT, D], F32).ap()
    wm_dram = nc.dram_tensor("wm_scratch", [P, CT, D], F32).ap()
    wc_dram = nc.dram_tensor("wc_scratch", [P, CT, D], F32).ap()

    with ExitStack() as ctx:
        def sb(name, shape, dt):
            return ctx.enter_context(nc.sbuf_tensor(name, shape, dt))

        def sem(name):
            return ctx.enter_context(nc.semaphore(name))

        KW = 256
        R1 = sb("region_t", [P, 64 * KW], F32R)
        R2 = sb("region_n", [P, 64 * KW], F32R)
        R3 = sb("region_l", [P, 20 * KW], F32R)
        F = sb("region_f", [P, 48 * KW], F32)
        prob = sb("prob", [P, M], F32)
        am_out = sb("am_out", [P, C], F32)
        max_part = sb("max_part", [P, MB], F32)
        row_max = sb("row_max", [P, 1], F32)
        neg_max = sb("neg_max", [P, 1], F32)
        sum_part = sb("sum_part", [P, MB], F32)
        row_sum = sb("row_sum", [P, 1], F32)
        row_inv = sb("row_inv", [P, 1], F32)
        sq_sum = sb("sq_sum", [P, 1], F32)
        mean_sq = sb("mean_sq", [P, 1], F32)
        rstd = sb("rstd", [P, 1], F32)
        m_half = sb("minus_half", [P, 1], F32)

        a_xt = R1[:, 32 * KW:64 * KW].rearrange("p (h t n) -> p h t n", h=2, t=DT)
        a_w = R2[:, 0:32 * KW].rearrange("p (h t c) -> p h t c", h=2, t=DT)
        a_q = R2[:, 32 * KW:48 * KW].rearrange("p (u c h n) -> p u c h n", u=TPB, c=CT, h=2)
        a_in = F[:, 0:16 * KW]
        a_tf = F[:, 16 * KW:32 * KW]
        a_wf = F[:, 32 * KW:48 * KW].rearrange("p (t c) -> p t c", t=DT)
        a_ef = F[:, 32 * KW:48 * KW]
        a_wc = prob[:].rearrange("p (c n) -> p c n", c=CT)
        b_mt = R1[:, :].rearrange("p (j h t m) -> p j h t m", j=MB, h=2, t=CT)
        b_mn = R2[:, :].rearrange("p (j h s c) -> p j h s c", j=MB, h=2, s=TPB)
        b_pt = R3[:, 0:16 * KW].rearrange("p (h k n) -> p h k n", h=2, k=MB * TPB)
        b_q = R3[:, 16 * KW:20 * KW].rearrange("p (c h n) -> p c h n", c=CT, h=2)
        b_q1 = R3[:, 12 * KW:16 * KW].rearrange("p (c h n) -> p c h n", c=CT, h=2)
        b_in = [F[:, 8 * KW * s:8 * KW * (s + 1)] for s in range(4)]
        b_tf = [F[:, 4 * KW * s:4 * KW * (s + 1)] for s in (8, 9, 0, 1, 2, 3, 4, 5)]
        MN_SLOT = (3, 0, 1, 2)
        b_px = F[:, 40 * KW:48 * KW]
        c_wg1 = R1[:, :].rearrange("p (t h d) -> p t h d", t=DT, h=2)
        c_xl0 = c_wg1[:, DT - 1, LO]
        c_wc = R2[:, 0:32 * KW].rearrange("p (t h d) -> p t h d", t=CT, h=2)
        c_wm = R2[:, 32 * KW:64 * KW].rearrange("p (t h d) -> p t h d", t=CT, h=2)
        c_xt = [R3[:, 16 * KW:20 * KW], R3[:, 0:4 * KW]]
        c_at = [R3[:, 4 * KW:6 * KW], R3[:, 6 * KW:8 * KW]]
        f_tile = [F[:, 4 * KW * s:4 * KW * (s + 1)] for s in range(12)]
        f_wg1 = f_tile[0:8]
        f_wcm = f_tile[1:8] + f_tile[10:11]
        c_ain, c_atf = F[:, 0:2 * KW], F[:, 2 * KW:4 * KW]
        c_z, c_u, c_out, c_xres, c_sq = f_tile[1:6]
        c_xin, c_xtf = f_tile[8:10]
        c_bias, c_nw = prob[:, 0:D], prob[:, D:2 * D]

        bank = [ctx.enter_context(nc.psum_tensor(f"bank{i}", [P, BANK], F32)) for i in range(7)]
        ps_t = bank[4:6]
        ps_am = bank[6]
        ps_z, ps_c = bank[0:2], bank[2:4]

        const_ready = sem("const_ready")
        w_loaded, g0_loaded = [sem(f"w_loaded{h}") for h in range(2)], [sem(f"g0_loaded{h}") for h in range(2)]
        w_hi, w_ready, g0_tile_t = sem("w_hi"), sem("w_ready"), sem("g0_tile_t")
        g1_half_loaded, g1_half_t = sem("g1_half_loaded"), sem("g1_half_t")
        x0_tile_hi, x0_tile_ready = sem("x0_tile_hi"), sem("x0_tile_ready")
        item_loaded, item_t = sem("item_loaded"), sem("item_t")
        xt_hi, xt_ready = sem("xt_hi"), sem("xt_ready")
        wt_stored = sem("wt_stored")
        q_half, q_done = sem("q_half"), sem("q_done")
        q_hi, q_ready = sem("q_hi"), sem("q_ready")
        wc_stored, q_stored = sem("wc_stored"), sem("q_stored")
        mt_loaded = [sem(f"mt_loaded{j}") for j in range(MB)]
        mn_loaded = [sem(f"mn_loaded{j}") for j in range(MB)]
        mt_t, mt_hi, mt_ready = sem("mt_t"), sem("mt_hi"), sem("mt_ready")
        mn_hi, mn_ready = sem("mn_hi"), sem("mn_ready")
        uq_loaded, q1_loaded = sem("uq_loaded"), sem("q1_loaded")
        s_done, max_done, max_all, neg_ready = sem("s_done"), sem("max_done"), sem("max_all"), sem("neg_ready")
        exp_done, sum_done, inv_done = sem("exp_done"), sem("sum_done"), sem("inv_done")
        p_stored = [sem(f"p_stored{j}") for j in range(MB)]
        px_loaded = sem("px_loaded")
        pt_t, pt_hi, pt_ready = sem("pt_t"), sem("pt_hi"), sem("pt_ready")
        av_done, am_ready, am_stored = sem("av_done"), sem("am_ready"), sem("am_stored")
        wg1_loaded = [sem(f"wg1_loaded{t}") for t in range(DT)]
        wcm_loaded = [sem(f"wcm_loaded{t}") for t in range(2 * CT)]
        wg1_hi, wg1_ready, wcm_hi, wcm_ready = sem("wg1_hi"), sem("wg1_ready"), sem("wcm_hi"), sem("wcm_ready")
        vec_loaded = sem("vec_loaded")
        xin_loaded, ain_loaded, xres_loaded = sem("xin_loaded"), sem("ain_loaded"), sem("xres_loaded")
        cx0_early_ready = sem("cx0_early_ready")
        cx_t, cx_hi, cx_ready, cx_used = sem("cx_t"), sem("cx_hi"), sem("cx_ready"), sem("cx_used")
        ca_t, ca_hi, ca_ready = sem("ca_t"), sem("ca_hi"), sem("ca_ready")
        z_done, z_biased, gate_done = sem("z_done"), sem("z_biased"), sem("gate_done")
        c_done, mul_done, fused_done = sem("c_done"), sem("mul_done"), sem("fused_done")
        sq_done, var_done, rstd_done = sem("sq_done"), sem("var_done"), sem("rstd_done")
        out_ready, out_stored = sem("out_ready"), sem("out_stored")

        HEAD = ("G0", "G1", "X0", "E0", "X1", "X2", "E1", "X3", "X4", "E2")
        HEAD_BLOCKS = tuple(name for name in HEAD if name[0] != "E")
        NHB = len(HEAD_BLOCKS)
        NHX = NHB - GB
        NBLOCKS = GB + NBLK

        def item_of_x(n):
            return n + len(HEAD) - NHX

        def load_quadrants(eng, dst, src, width, signal, part=(0, 1)):
            chunk = width // NQ
            lo, hi = chunk // part[1] * part[0], chunk // part[1] * (part[0] + 1)
            v = dst.rearrange("p (b f) -> p b f", f=chunk)
            for q in range(NQ):
                eng.dma_start(v[SQ * q:SQ * (q + 1), :, lo:hi],
                              src[:, chunk * q + lo:chunk * q + hi].rearrange("(b i) f -> i b f", i=SQ)
                              ).then_inc(signal, 16)

        def transpose_blocks(dst, src, tiles, part=(0, 1)):
            ts = slice(tiles // part[1] * part[0], tiles // part[1] * (part[0] + 1))
            return nc.vector.transpose(dst.rearrange("p (t b i) -> p t b i", t=tiles, i=SQ)[:, ts],
                                       src.rearrange("p (b t j) -> p t b j", t=tiles, j=SQ)[:, ts])

        HT = DT // 2

        def tile_count(own, halves, t):
            return (halves, t // HT + 1) if t % HT == HT - 1 else (own, t - t // HT + 1)

        def tile_of_tf(t):
            return a_tf[:, BANK * t:BANK * (t + 1)]

        def w_quarter(half, c):
            ts = slice(DT // 2 * half, DT // 2 * (half + 1))
            return (a_wf.rearrange("p t (q c j) -> p t c q j", q=NQ, j=SQ)[:, ts, c],
                    *(a_w[:, part, ts, P * c:P * (c + 1)].rearrange("p t (q j) -> p t q j", q=NQ)
                      for part in (HI, LO)))

        HPJ = 2
        MTS = MB * HPJ
        WG1_EARLY = 5
        MN_FIRST = 2
        MN_EARLY = 2

        def mt_half(part, h):
            w = BANK // HPJ
            return b_mt[:, h // HPJ, part, :, w * (h % HPJ):w * (h % HPJ + 1)]

        def tf_half(h):
            return b_tf[h].rearrange("p (t m) -> p t m", t=CT)

        def minus_hi(dst, src, hi):
            return nc.vector.tensor_tensor(dst, src, hi.bitcast(F32), ALU.subtract)

        block = ctx.enter_context(nc.Block())

        @block.sync
        def _(sp):
            for h in range(2):
                for q in range(NQ):
                    sp.dma_start(a_wf[SQ * q:SQ * (q + 1), DT // 2 * h:DT // 2 * (h + 1)],
                                 w_mem[CHX * q + CHX // 2 * h:CHX * q + CHX // 2 * (h + 1), :].rearrange(
                                     "(t j) c -> j t c", j=SQ)).then_inc(w_loaded[h], 16)
                load_quadrants(sp, a_in, w_gate[0:BANK, D:2 * D], D, g0_loaded[h], part=(h, 2))

            def load_item(name, n):
                sp.wait_ge(item_t, n)
                k = int(name[1])
                if name[0] == "G":
                    load_quadrants(sp, a_in, w_gate[BANK * k:BANK * (k + 1), D:2 * D], D, item_loaded)
                elif name[0] == "X":
                    load_quadrants(sp, a_in, x_rows[BANK * k:BANK * (k + 1), :], D, item_loaded)
                elif name == "E2":
                    load_quadrants(sp, a_in, w_mem, C, item_loaded)
                else:
                    load_quadrants(sp, a_in, w_gate[BANK * k:BANK * (k + 1), 0:D], D, item_loaded)

            def store_wt(e):
                sp.wait_ge(item_t, HEAD.index(f"E{e}") + 1)
                if e < 2:
                    sp.dma_start(wg1_dram[:, :, BANK * e:BANK * (e + 1)],
                                 a_ef.rearrange("p (t n) -> p t n", t=DT)).then_inc(wt_stored, 16)
                else:
                    sp.dma_start(wm_dram, a_ef.rearrange("p (t n) -> p t n", t=CT)).then_inc(wt_stored, 16)

            def store_wc(k):
                sp.wait_ge(q_ready, CT * (k + 1))
                sp.dma_start(wc_dram[:, :, BANK * k:BANK * (k + 1)], a_wc).then_inc(wc_stored, 16)

            def store_q(n):
                sp.wait_ge(q_ready, (n + (GB + 1)) * CT)
                sp.dma_start(q_dram[bass.ds(n * TPB, TPB)].rearrange("u p f -> p u f"),
                             a_q.bitcast(F32).rearrange("p u c h n -> p u (c h n)")).then_inc(q_stored, 16)

            g1 = w_gate[BANK:2 * BANK, D:2 * D]
            sp.wait_ge(g0_tile_t, HT)
            load_quadrants(sp, a_in, g1, D, g1_half_loaded, part=(0, 2))
            sp.wait_ge(item_t, 1)
            load_quadrants(sp, a_in, g1, D, item_loaded, part=(1, 2))
            load_item("X0", 2)
            load_item("E0", 3)
            store_wc(0)
            load_item("X1", 4)
            store_wt(0)
            store_wc(1)
            load_item("X2", 5)
            store_q(0)
            load_item("E1", 6)
            load_item("X3", 7)
            store_q(1)
            store_wt(1)
            load_item("X4", 8)
            store_q(2)
            load_item("E2", 9)
            load_item(f"X{NHX}", len(HEAD))
            store_q(NHX - 2)
            store_wt(2)
            with sp.Fori(NHX + 1, NBLK) as n:
                sp.wait_ge(item_t, n + item_of_x(0))
                load_quadrants(sp, a_in, x_rows[bass.ds(n * BANK, BANK), :], D, item_loaded)
                store_q(n - 2)

            def load_mt(b, j):
                load_quadrants(sp, b_in[j], mem[b, BANK * j:BANK * (j + 1), :], C, mt_loaded[j])

            def load_mn(b, j):
                v = b_in[MN_SLOT[j]].rearrange("p (s c) -> p s c", s=TPB)
                for q in range(NQ):
                    r = M // NQ * q + P * j
                    sp.dma_start(v[SQ * q:SQ * (q + 1)],
                                 mem[b, r:r + P, :].rearrange("(s i) c -> i s c", i=SQ)).then_inc(mn_loaded[j], 16)

            def load_q(unit, dst=b_q, signal=uq_loaded):
                sp.dma_start(dst.bitcast(F32).rearrange("p c h n -> p (c h n)"), q_dram[unit]).then_inc(signal, 16)

            def store_am(i):
                sp.wait_ge(am_ready, i + 1)
                v = am_dram[i].rearrange("(q i) (b c) -> b i q c", q=NQ, b=TPB)
                for b in range(TPB):
                    sp.dma_start(v[b], am_out[SQ * b:SQ * (b + 1), :].rearrange("i (q c) -> i q c", q=NQ)
                                 ).then_inc(am_stored, 16)

            sp.wait_ge(item_t, item_of_x(NBLK))
            load_mt(0, 0)
            load_mt(0, 1)
            store_q(NBLK - 2)
            sp.wait_ge(xt_ready, 2 * NBLOCKS)
            load_mt(0, 2)
            load_mt(0, 3)
            sp.wait_ge(q_stored, 16 * (NBLK - 1))
            load_q(0)
            load_q(1, b_q1, q1_loaded)
            store_q(NBLK - 1)

            def mn_slot_free(b, j):
                if j == 0:
                    sp.wait_ge(mt_t, b * MTS + MTS)
                else:
                    sp.wait_ge(mt_ready, b * MTS + HPJ * (j + 1))


            def exchange(unit, first=False):
                def there(j):
                    sp.wait_ge(exp_done, unit * MB + j + 1)
                    cols = slice(BANK * j, BANK * (j + 1))
                    sp.dma_start(prob_dram[unit, :, cols], prob[:, cols]).then_inc(p_stored[j], 16)

                def back(j):
                    sp.wait_ge(p_stored[j], (unit + 1) * 16)
                    if j == 0 and not first:
                        sp.wait_ge(pt_t, unit * MB)
                    sp.dma_start(b_px[SQ * j:SQ * (j + 1)].rearrange("i (b m) -> i b m", b=TPB),
                                 prob_dram[unit, :, BANK * j:BANK * (j + 1)].rearrange("(b i) m -> i b m", i=SQ)
                                 ).then_inc(px_loaded, 16)

                there(0)
                there(1)
                for j in range(2, MB):
                    there(j)
                    back(j - 2)
                back(MB - 2)
                back(MB - 1)

            for j in range(MN_FIRST):
                mn_slot_free(0, j)
                load_mn(0, j)
            exchange(0, first=True)
            for j in range(MN_FIRST, MB):
                mn_slot_free(0, j)
                load_mn(0, j)

            def step_sp(i, unit_after_next=True, softmax=True):
                if unit_after_next:
                    sp.wait_ge(s_done, (i + 2) * MB)
                    load_q(i + 2)
                if softmax:
                    exchange(i + 1)
                store_am(i)

            def load_next_mt(b, j):
                sp.wait_ge(mn_ready, (b + 1) * MB)
                load_mt(b + 1, j)

            def load_next_mn(b, j):
                mn_slot_free(b + 1, j)
                load_mn(b + 1, j)

            sp.wait_ge(q_stored, 16 * NBLK)
            step_sp(0)
            with sp.Fori(0, NB - 1) as b:
                for j in range(MB):
                    if j < 2:
                        step_sp(b * UPB + 1 + j)
                    load_next_mt(b, j)
                with sp.Fori(3, 6) as u:
                    step_sp(b * UPB + u)
                load_next_mn(b, 0)
                sp.wait_ge(s_done, (b * UPB + 8) * MB)
                load_q(b * UPB + 8)
                exchange(b * UPB + 7)
                for j in range(1, MB):
                    load_next_mn(b, j)
                store_am(b * UPB + 6)
                step_sp(b * UPB + 7)
                step_sp(b * UPB + 8)
            LB = (NB - 1) * UPB

            sp.wait_ge(mn_ready, NB * MB)
            sp.wait_ge(wt_stored, 3 * 16)
            sp.wait_ge(wc_stored, GB * 16)
            load_quadrants(sp, c_xin, x_rows[0:P, :], D, xin_loaded)
            for u in range(1, 6):
                step_sp(LB + u)
                if u < 5:
                    for t in (2 * u - 2, 2 * u - 1):
                        sp.dma_start(f_wg1[t], wg1_dram[:, t]).then_inc(wg1_loaded[t], 16)
            exchange(NUNIT - 1)
            sp.wait_ge(wg1_ready, 1)
            sp.dma_start(c_ain, am_dram[0]).then_inc(ain_loaded, 16)
            store_am(NUNIT - 2)
            for t in range(2 * CT):
                if t < 2 * CT - 1:
                    sp.wait_ge(wg1_ready, t + 2)
                else:
                    sp.wait_ge(pt_t, NUNIT * MB)
                sp.dma_start(f_wcm[t], (wc_dram if t < CT else wm_dram)[:, t % CT]).then_inc(wcm_loaded[t], 16)
            for j in range(MB):
                sp.wait_ge(p_stored[j], 16 * NUNIT)
            sp.dma_start(c_bias, b_gate.rearrange("(a d) -> a d", a=1).to_broadcast([P, D])).then_inc(vec_loaded, 16)
            sp.dma_start(c_nw, norm_w.rearrange("(a d) -> a d", a=1).to_broadcast([P, D])).then_inc(vec_loaded, 16)
            store_am(NUNIT - 1)

            def load_inputs(k):
                sp.wait_ge(cx_t, k)
                load_quadrants(sp, c_xin, x_rows[bass.ds(k * P, P), :], D, xin_loaded)
                sp.wait_ge(ca_t, k)
                sp.dma_start(c_ain, am_dram[k]).then_inc(ain_loaded, 16)

            def store_out(k):
                sp.wait_ge(out_ready, k + 1)
                sp.dma_start(out_rows[bass.ds(k * P, P), :], c_out).then_inc(out_stored, 16)

            def next_residual(k):
                sp.wait_ge(fused_done, k + 1)
                sp.dma_start(c_xres, x_rows[bass.ds(k * P + P, P), :]).then_inc(xres_loaded, 16)

            load_inputs(1)
            sp.wait_ge(wcm_ready, CT)
            sp.dma_start(c_xres, x_rows[0:P, :]).then_inc(xres_loaded, 16)
            sp.wait_ge(am_stored, 64 * NUNIT)
            with sp.Fori(0, NUNIT - 2) as k:
                load_inputs(k + 2)
                next_residual(k)
                store_out(k)
            next_residual(NUNIT - 2)
            store_out(NUNIT - 2)
            for h in range(DH):
                sp.wait_ge(out_ready, NUNIT + h)
                cols = slice(BANK * h, BANK * (h + 1))
                sp.dma_start(out_rows[ROWS - P:ROWS, cols], c_out[:, cols]).then_inc(out_stored, 16)
            sp.wait_ge(out_stored, 16 * (NUNIT - 1 + DH))

        @block.gpsimd
        def _(pool):
            nc.gpsimd.memset(m_half[:], -0.5).then_inc(const_ready, 1)
            pool.wait_ge(const_ready, 1)
            with pool.Fori(0, NUNIT) as k:
                pool.wait_ge(var_done, k + 1)
                nc.gpsimd.tensor_tensor(rstd[:], mean_sq[:], m_half[:], ALU.pow).then_inc(rstd_done, 1)

        @block.scalar
        def _(act):
            def split_w(half):
                act.wait_ge(w_loaded[half], 16 * NQ)
                for c in range(CT):
                    src, hi, _ = w_quarter(half, c)
                    nc.scalar.copy(hi, src).then_inc(w_hi, 1)

            def split_half(half):
                n = DT // 2 * BANK
                nc.scalar.copy(a_xt[:, HI, DT // 2 * half:DT // 2 * (half + 1), :].rearrange("p t n -> p (t n)"),
                               a_tf[:, n * half:n * (half + 1)]).then_inc(xt_hi, 1)

            def evacuate_q(k, free):
                free()
                for c in range(CT):
                    act.wait_ge(q_done, k * CT + c + 1)
                    nc.scalar.copy(a_q[:, :, c, HI, :], bank[c][:].rearrange("p (u n) -> p u n", u=TPB)
                                   ).then_inc(q_hi, 1)

            def evacuate_wc(k):
                if k > 0:
                    act.wait_ge(wc_stored, 16 * k)
                for c in range(CT):
                    act.wait_ge(q_done, k * CT + c + 1)
                    nc.scalar.copy(a_wc[:, c], bank[c][:]).then_inc(q_ready, 1)
                if k == 0:
                    act.wait_ge(item_t, 2)

            split_w(0)
            for t in range(DT):
                if t == HT:
                    split_w(1)
                act.wait_ge(*((g0_tile_t, t + 1) if t < DT - 1 else (item_t, 1)))
                signal, _ = tile_count(x0_tile_hi, xt_hi, t)
                nc.scalar.copy(a_xt[:, HI, t, :], tile_of_tf(t)).then_inc(signal, 1)
            for k in range(NHB - 1):
                item = HEAD.index(HEAD_BLOCKS[k + 1])
                if k == 0:
                    act.wait_ge(g1_half_t, 1)
                else:
                    act.wait_ge(item_t, item + 1)
                act.wait_ge(q_half, k + 1)
                split_half(0)
                if k < GB:
                    evacuate_wc(k)
                elif k == GB:
                    evacuate_q(k, lambda: None)
                else:
                    evacuate_q(k, lambda: act.wait_ge(q_stored, 16 * (k - GB)))
                split_half(1)
            with act.Fori(NHB - 1, NBLOCKS - 1) as k:
                act.wait_ge(item_t, k + (item_of_x(0) - GB) + 2)
                act.wait_ge(q_half, k + 1)
                split_half(0)
                evacuate_q(k, lambda: act.wait_ge(q_stored, (k - GB) * 16))
                split_half(1)

            def mt_split(b, halves):
                for h in halves:
                    act.wait_ge(mt_t, b * MTS + h + 1)
                    nc.scalar.copy(mt_half(HI, h), tf_half(h)).then_inc(mt_hi, 1)

            def mn_split(b, j):
                act.wait_ge(mn_loaded[j], (b + 1) * (16 * NQ))
                nc.scalar.copy(b_mn[:, j, HI].rearrange("p s c -> p (s c)"), b_in[MN_SLOT[j]]).then_inc(mn_hi, 1)

            def exps(unit, stored=True):
                act.wait_ge(neg_ready, unit + 1)
                if stored:
                    for j in range(MB):
                        act.wait_ge(p_stored[j], unit * 16)
                for j in range(MB):
                    nc.scalar.activation(prob[:, BANK * j:BANK * (j + 1)], bank[j][:], ACT.Exp, bias=neg_max[:],
                                         scale=SCALE, accum_out=sum_part[:, j:j + 1]).then_inc(exp_done, 1)

            def wg1_split(tiles):
                for t in tiles:
                    act.wait_ge(wg1_loaded[t], 16)
                    nc.scalar.copy(c_wg1[:, t, HI], f_wg1[t]).then_inc(wg1_hi, 1)

            def step_act(i, mn_of=None, mt_of=None, mn_next=None, softmax=True, first=False, weights=False):
                if mn_of is not None and first:
                    act.wait_ge(q_done, NBLOCKS * CT)
                    for g in range(MN_FIRST):
                        mn_split(mn_of, g)
                for g in range(MB):
                    if mn_of is not None and g >= (MN_FIRST if first else MN_EARLY):
                        if not first:
                            act.wait_ge(av_done, (mn_of * UPB - 1) * MB + g + 1)
                        mn_split(mn_of, g)
                    act.wait_ge(pt_t, i * MB + g + 1)
                    nc.scalar.copy(b_pt[:, HI, TPB * g:TPB * (g + 1), :].rearrange("p k n -> p (k n)"),
                                   ps_t[g % 2][:]).then_inc(pt_hi, 1)
                if mt_of is not None:
                    act.wait_ge(s_done, (mt_of * UPB) * MB)
                    mt_split(mt_of, range(0, MTS // 2))
                if weights:
                    act.wait_ge(s_done, NUNIT * MB)
                    wg1_split(range(0, DT // 2))
                    act.wait_ge(cx_t, 1)
                    nc.scalar.copy(c_xt[HI], c_xtf).then_inc(cx_hi, 1)
                if softmax:
                    act.wait_ge(sum_done, i + 1)
                    exps(i + 1)
                if mt_of is not None:
                    mt_split(mt_of, range(MTS // 2, MTS))
                if weights:
                    wg1_split(range(DT // 2, DT))
                if mn_next is not None:
                    for g in range(MN_EARLY):
                        act.wait_ge(av_done, (mn_next * UPB - 1) * MB + g + 1)
                        mn_split(mn_next, g)

            mt_split(0, range(0, MTS // 2))
            evacuate_q(NBLOCKS - 1, lambda: act.wait_ge(q_stored, 16 * (NBLK - 1)))
            mt_split(0, range(MTS // 2, MTS))
            exps(0, stored=False)
            act.wait_ge(q_stored, 16 * NBLK)
            step_act(0, mn_of=0, first=True)
            with act.Fori(0, NB - 1) as b:
                with act.Fori(1, 6) as u:
                    step_act(b * UPB + u)
                step_act(b * UPB + 6, mt_of=b + 1)
                step_act(b * UPB + 7, mn_next=b + 1)
                step_act(b * UPB + 8, mn_of=b + 1)
            LB = (NB - 1) * UPB
            with act.Fori(1, 6) as u:
                step_act(LB + u)
            step_act(LB + 6, weights=True)
            step_act(LB + 7, softmax=False)

            def split_x(k):
                act.wait_ge(cx_t, k + 1)
                nc.scalar.copy(c_xt[HI], c_xtf).then_inc(cx_hi, 1)

            def split_am(k):
                act.wait_ge(ca_t, k + 1)
                nc.scalar.copy(c_at[HI], c_atf).then_inc(ca_hi, 1)

            def unit_act(k, following=True):
                if following:
                    act.wait_ge(cx_used, k + 1)
                    split_x(k + 1)
                for h in range(DH):
                    act.wait_ge(z_biased, k * DH + h + 1)
                    v = c_z[:, BANK * h:BANK * (h + 1)]
                    nc.scalar.activation(v, v, ACT.Sigmoid).then_inc(gate_done, 1)
                if following:
                    act.wait_ge(c_done, k * DH + DH)
                    split_am(k + 1)

            def wcm_tile(part, t):
                return (c_wc if t < CT else c_wm)[:, t % CT, part]

            for t in range(2 * CT):
                if t == CT:
                    act.wait_ge(av_done, NUNIT * MB)
                    split_am(0)
                act.wait_ge(av_done, (NUNIT - 1) * MB + t // 2 + 1)
                act.wait_ge(wcm_loaded[t], 16)
                nc.scalar.copy(wcm_tile(HI, t), f_wcm[t]).then_inc(wcm_hi, 1)
            with act.Fori(0, NUNIT - 1) as k:
                unit_act(k)
            unit_act(NUNIT - 1, following=False)

        @block.vector
        def _(dve):
            def split_w(half):
                for c in range(CT):
                    dve.wait_ge(w_hi, half * CT + c + 1)
                    src, hi, lo = w_quarter(half, c)
                    minus_hi(lo, src, hi).then_inc(w_ready, 1)

            def transpose_item(count, dst=a_tf, tiles=DT):
                dve.wait_ge(item_loaded, (count - 1) * (16 * NQ))
                transpose_blocks(dst, a_in, tiles).then_inc(item_t, 1)

            def split_half(count, half):
                dve.wait_ge(xt_hi, count)
                n = DT // 2 * BANK
                sl = slice(DT // 2 * half, DT // 2 * (half + 1))
                minus_hi(a_xt[:, LO, sl, :].rearrange("p t n -> p (t n)"), a_tf[:, n * half:n * (half + 1)],
                         a_xt[:, HI, sl, :].rearrange("p t n -> p (t n)")).then_inc(xt_ready, 1)

            def evacuate_q(k, between=lambda c: None):
                for c in range(CT):
                    between(c)
                    dve.wait_ge(q_hi, (k - GB) * CT + c + 1)
                    minus_hi(a_q[:, :, c, LO, :], bank[c][:].rearrange("p (u n) -> p u n", u=TPB),
                             a_q[:, :, c, HI, :]).then_inc(q_ready, 1)

            for half in range(2):
                split_w(half)
                dve.wait_ge(g0_loaded[half], 16 * NQ)
                tiles = range(HT * half, HT * (half + 1))

                def transpose_tile(t):
                    transpose_blocks(a_tf, a_in, DT, part=(t, DT)).then_inc(g0_tile_t if t < DT - 1 else item_t, 1)

                transpose_tile(tiles[0])
                for t in tiles:
                    if t + 1 in tiles:
                        transpose_tile(t + 1)
                    dve.wait_ge(*tile_count(x0_tile_hi, xt_hi, t))
                    signal, _ = tile_count(x0_tile_ready, xt_ready, t)
                    minus_hi(a_xt[:, LO, t, :], tile_of_tf(t), a_xt[:, HI, t, :]).then_inc(signal, 1)
            for k in range(NHB - 1):
                item = HEAD.index(HEAD_BLOCKS[k + 1])
                if k == 0:
                    dve.wait_ge(xt_ready, 1)
                    dve.wait_ge(g1_half_loaded, 16 * NQ)
                    transpose_blocks(a_tf, a_in, DT, part=(0, 2)).then_inc(g1_half_t, 1)
                    split_half(3, 0)
                    dve.wait_ge(xt_ready, 2)
                    dve.wait_ge(item_loaded, 16 * NQ)
                    transpose_blocks(a_tf, a_in, DT, part=(1, 2)).then_inc(item_t, 1)
                else:
                    dve.wait_ge(xt_ready, 2 * (k + 1))
                    transpose_item(item + 1)
                    split_half(2 * k + 3, 0)

                def transpose_weights(c):
                    if c == 2 and item + 1 < len(HEAD) and HEAD[item + 1][0] == "E":
                        e = int(HEAD[item + 1][1])
                        if e > 0:
                            dve.wait_ge(wt_stored, 16 * e)
                        else:
                            dve.wait_ge(w_ready, 2 * CT)
                        transpose_item(item + 2, a_ef, CT if e == 2 else DT)

                if k < GB:
                    transpose_weights(2)
                else:
                    evacuate_q(k, transpose_weights)
                split_half(2 * k + 4, 1)
            with dve.Fori(NHB - 1, NBLOCKS - 1) as k:
                dve.wait_ge(xt_ready, k * 2 + 2)
                transpose_item(k + (item_of_x(0) - GB) + 2)
                split_half(k * 2 + 3, 0)
                evacuate_q(k)
                split_half(k * 2 + 4, 1)

            def mt_transpose(b, h):
                dve.wait_ge(mt_loaded[h // HPJ], (b + 1) * (16 * NQ))
                if h >= 2:
                    dve.wait_ge(mt_t, b * MTS + h // HPJ * HPJ)
                rows = b_in[h // HPJ].rearrange("p (b t j) -> p t b j", t=CT, j=SQ)
                nb = BANK // SQ // HPJ
                nc.vector.transpose(tf_half(h).rearrange("p t (b i) -> p t b i", i=SQ),
                                    rows[:, :, nb * (h % HPJ):nb * (h % HPJ + 1)]).then_inc(mt_t, 1)

            def mt_split(b, h):
                dve.wait_ge(mt_hi, b * MTS + h + 1)
                minus_hi(mt_half(LO, h), tf_half(h), mt_half(HI, h)).then_inc(mt_ready, 1)

            def mn_split(b, j):
                dve.wait_ge(mn_hi, b * MB + j + 1)
                minus_hi(b_mn[:, j, LO].rearrange("p s c -> p (s c)"), b_in[MN_SLOT[j]],
                         b_mn[:, j, HI].rearrange("p s c -> p (s c)")).then_inc(mn_ready, 1)

            def block_max(unit, j):
                dve.wait_ge(s_done, unit * MB + j + 1)
                nc.vector.reduce_max(max_part[:, j:j + 1], bank[j][:], AX_X).then_inc(max_done, 1)

            def unit_max(unit):
                dve.wait_ge(max_done, unit * MB + MB)
                nc.vector.reduce_max(row_max[:], max_part[:], AX_X).then_inc(max_all, 1)
                dve.wait_ge(max_all, unit + 1)
                nc.vector.tensor_scalar(neg_max[:], row_max[:], -SCALE, None, ALU.mult).then_inc(neg_ready, 1)

            def unit_sum(unit):
                dve.wait_ge(exp_done, unit * MB + MB)
                nc.vector.reduce_sum(row_sum[:], sum_part[:], AX_X).then_inc(sum_done, 1)

            def unit_inverse(unit):
                dve.wait_ge(sum_done, unit + 1)
                nc.vector.reciprocal(row_inv[:], row_sum[:]).then_inc(inv_done, 1)

            def normalise_am(i, stored):
                dve.wait_ge(av_done, i * MB + MB)
                if stored:
                    dve.wait_ge(am_stored, i * 64)
                dve.wait_ge(inv_done, i + 1)
                nc.vector.tensor_scalar(am_out[:], ps_am[:], row_inv[:], None, ALU.mult).then_inc(am_ready, 1)

            def pt_transpose(i, g):
                if g >= 2:
                    dve.wait_ge(pt_ready, i * MB + g - 1)
                v = b_px.rearrange("p (b k j) -> p k b j", b=TPB, j=SQ)
                nc.vector.transpose(ps_t[g % 2][:].rearrange("p (k b i) -> p k b i", k=TPB, i=SQ),
                                    v[:, TPB * g:TPB * (g + 1)]).then_inc(pt_t, 1)

            def transpose_x(k):
                dve.wait_ge(xin_loaded, (k + 1) * (16 * NQ))
                transpose_blocks(c_xtf, c_xin, DT).then_inc(cx_t, 1)

            def split_wg1(tiles):
                for t in tiles:
                    dve.wait_ge(wg1_hi, t + 1)
                    minus_hi(c_wg1[:, t, LO], f_wg1[t], c_wg1[:, t, HI]).then_inc(wg1_ready, 1)

            def step_dve(i, mn_of=None, mt_ahead=None, mt_of=None, mn_next=None, softmax=True, stored=True,
                         weights=False, last=False):
                dve.wait_ge(px_loaded, (i + 1) * (16 * NQ))
                if stored:
                    dve.wait_ge(av_done, i * MB)
                pt_transpose(i, 0)
                for g in range(MB):
                    if g + 1 < MB:
                        pt_transpose(i, g + 1)
                    if softmax:
                        block_max(i + 1, g)
                    if not stored and g == MB // 2:
                        dve.wait_ge(s_done, 2 * MB)
                    dve.wait_ge(pt_hi, i * MB + g + 1)
                    minus_hi(b_pt[:, LO, TPB * g:TPB * (g + 1), :].rearrange("p k n -> p (k n)"), ps_t[g % 2][:],
                             b_pt[:, HI, TPB * g:TPB * (g + 1), :].rearrange("p k n -> p (k n)")
                             ).then_inc(pt_ready, 1)
                    if mn_of is not None and g >= (MN_EARLY if stored else MN_FIRST):
                        mn_split(mn_of, g)
                if softmax:
                    unit_max(i + 1)
                if mt_ahead is not None:
                    for h in mt_ahead[1]:
                        mt_transpose(mt_ahead[0], h)
                if mt_of is not None:
                    for h in range(MTS):
                        mt_split(mt_of, h)
                if weights:
                    transpose_x(0)
                    split_wg1(range(0, WG1_EARLY - 1))
                    dve.wait_ge(cx_hi, 1)
                    early = slice(0, P * WG1_EARLY)
                    minus_hi(c_xl0[:, early], c_xtf[:, early], c_xt[HI][:, early]).then_inc(cx0_early_ready, 1)
                    split_wg1(range(WG1_EARLY - 1, WG1_EARLY))
                if softmax:
                    dve.wait_ge(inv_done, i + 1)
                    unit_sum(i + 1)
                if mn_next is not None:
                    for g in range(MN_EARLY):
                        mn_split(mn_next, g)
                if not last:
                    normalise_am(i, stored)
                if softmax:
                    dve.wait_ge(am_ready, i + 1)
                    unit_inverse(i + 1)

            dve.wait_ge(wt_stored, 3 * 16)
            for h in range(MTS // 2):
                mt_transpose(0, h)
            for h in range(MTS // 2):
                mt_split(0, h)
            dve.wait_ge(mt_ready, MTS // 2)

            def transpose_rest(c):
                if c > 0:
                    mt_transpose(0, MTS // 2 + c - 1)

            evacuate_q(NBLOCKS - 1, transpose_rest)
            mt_transpose(0, MTS - 1)
            for h in range(MTS // 2, MTS):
                mt_split(0, h)
            for j in range(MB):
                block_max(0, j)
            unit_max(0)
            unit_sum(0)
            unit_inverse(0)
            for g in range(MN_FIRST):
                mn_split(0, g)
            step_dve(0, mn_of=0, stored=False)
            with dve.Fori(0, NB - 1) as b:
                with dve.Fori(1, 4) as u:
                    step_dve(b * UPB + u)
                dve.wait_ge(mt_ready, b * MTS + MTS)
                step_dve(b * UPB + 4, mt_ahead=(b + 1, range(0, MTS // 2)))
                step_dve(b * UPB + 5, mt_ahead=(b + 1, range(MTS // 2, MTS)))
                step_dve(b * UPB + 6, mt_of=b + 1)
                step_dve(b * UPB + 7, mn_next=b + 1)
                step_dve(b * UPB + 8, mn_of=b + 1)
            LB = (NB - 1) * UPB
            with dve.Fori(1, 6) as u:
                step_dve(LB + u)
            step_dve(LB + 6, weights=True)

            def transpose_am(k):
                dve.wait_ge(ain_loaded, (k + 1) * 16)
                transpose_blocks(c_atf, c_ain, CT).then_inc(ca_t, 1)

            def split_x(k):
                dve.wait_ge(cx_hi, k + 1)
                minus_hi(c_xt[LO], c_xtf, c_xt[HI]).then_inc(cx_ready, 1)

            def split_am(k):
                dve.wait_ge(ca_hi, k + 1)
                minus_hi(c_at[LO], c_atf, c_at[HI]).then_inc(ca_ready, 1)

            def split_wcm(tiles):
                for t in tiles:
                    dve.wait_ge(wcm_hi, t + 1)
                    w = (c_wc if t < CT else c_wm)[:, t % CT]
                    minus_hi(w[:, LO], f_wcm[t], w[:, HI]).then_inc(wcm_ready, 1)

            step_dve(LB + 7, softmax=False, last=True)
            split_wg1(range(WG1_EARLY, DT - 1))
            late = slice(P * WG1_EARLY, P * DT)
            dve.wait_ge(av_done, (NUNIT - 1) * MB + MB // 2)
            minus_hi(c_xt[LO][:, late], c_xtf[:, late], c_xt[HI][:, late]).then_inc(cx_ready, 1)
            split_wg1(range(DT - 1, DT))
            transpose_am(0)
            split_wcm(range(0, CT))
            split_am(0)
            normalise_am(NUNIT - 1, stored=True)
            split_wcm(range(CT, 2 * CT))
            dve.wait_ge(vec_loaded, 32)

            def unit_dve(k, following=True, stored=True):
                if following:
                    dve.wait_ge(cx_ready, k + 1)
                    transpose_x(k + 1)
                    split_x(k + 1)
                for h in range(DH):
                    dve.wait_ge(z_done, k * DH + h + 1)
                    cols = slice(BANK * h, BANK * (h + 1))
                    nc.vector.tensor_tensor(c_z[:, cols], ps_z[h][:], c_bias[:, cols], ALU.add
                                            ).then_inc(z_biased, 1)
                if following:
                    dve.wait_ge(ca_ready, k + 1)
                    transpose_am(k + 1)
                for h in range(DH):
                    dve.wait_ge(gate_done, k * DH + h + 1)
                    dve.wait_ge(c_done, k * DH + h + 1)
                    if stored:
                        dve.wait_ge(out_ready, k)
                    cols = slice(BANK * h, BANK * (h + 1))
                    nc.vector.tensor_tensor(c_u[:, cols], ps_c[h][:], c_z[:, cols], ALU.mult).then_inc(mul_done, 1)
                if following:
                    split_am(k + 1)
                dve.wait_ge(mul_done, k * DH + DH)
                dve.wait_ge(xres_loaded, (k + 1) * 16)
                nc.vector.tensor_tensor(c_u, c_u, c_xres, ALU.add).then_inc(fused_done, 1)
                dve.wait_ge(fused_done, k + 1)
                nc.vector.tensor_tensor_reduce(out=c_sq, in0=c_u, in1=c_u, scale=1.0, scalar=0.0, op0=ALU.mult,
                                               op1=ALU.add, accum_out=sq_sum[:]).then_inc(sq_done, 1)
                dve.wait_ge(sq_done, k + 1)
                nc.vector.tensor_scalar(mean_sq[:], sq_sum[:], 1.0 / D, RMS_EPS, ALU.mult, ALU.add
                                        ).then_inc(var_done, 1)
                dve.wait_ge(rstd_done, k + 1)
                if stored:
                    dve.wait_ge(out_stored, k * 16)
                nc.vector.scalar_tensor_tensor(out=c_out, in0=c_u, scalar=rstd[:], in1=c_nw, op0=ALU.mult,
                                               op1=ALU.mult).then_inc(out_ready, 1)

            def last_unit_dve(k):
                halves = [slice(BANK * h, BANK * (h + 1)) for h in range(DH)]
                for h in range(DH):
                    dve.wait_ge(z_done, k * DH + h + 1)
                    nc.vector.tensor_tensor(c_z[:, halves[h]], ps_z[h][:], c_bias[:, halves[h]], ALU.add
                                            ).then_inc(z_biased, 1)
                dve.wait_ge(xres_loaded, (k + 1) * 16)
                dve.wait_ge(out_ready, k)
                for h in range(DH):
                    dve.wait_ge(gate_done, k * DH + h + 1)
                    dve.wait_ge(c_done, k * DH + h + 1)
                    u = c_u[:, halves[h]]
                    nc.vector.tensor_tensor(u, ps_c[h][:], c_z[:, halves[h]], ALU.mult).then_inc(mul_done, 1)
                    dve.wait_ge(mul_done, k * DH + h + 1)
                    nc.vector.tensor_tensor(u, u, c_xres[:, halves[h]], ALU.add).then_inc(fused_done, 1)
                    dve.wait_ge(fused_done, k + h + 1)
                    nc.vector.tensor_tensor_reduce(out=c_sq[:, halves[h]], in0=u, in1=u, scale=1.0, scalar=0.0,
                                                   op0=ALU.mult, op1=ALU.add, accum_out=sum_part[:, h:h + 1]
                                                   ).then_inc(sq_done, 1)
                dve.wait_ge(sq_done, k + DH)
                nc.vector.reduce_sum(sq_sum[:], sum_part[:, 0:DH], AX_X).then_inc(sq_done, 1)
                dve.wait_ge(sq_done, k + DH + 1)
                nc.vector.tensor_scalar(mean_sq[:], sq_sum[:], 1.0 / D, RMS_EPS, ALU.mult, ALU.add
                                        ).then_inc(var_done, 1)
                dve.wait_ge(rstd_done, k + 1)
                dve.wait_ge(out_stored, k * 16)
                for h in range(DH):
                    nc.vector.scalar_tensor_tensor(out=c_out[:, halves[h]], in0=c_u[:, halves[h]], scalar=rstd[:],
                                                   in1=c_nw[:, halves[h]], op0=ALU.mult, op1=ALU.mult
                                                   ).then_inc(out_ready, 1)

            unit_dve(0, stored=False)
            with dve.Fori(1, NUNIT - 1) as k:
                unit_dve(k)
            last_unit_dve(NUNIT - 1)

        @block.tensor
        def _(pe):
            def product(dst, lhs, rhs, first, last):
                for n, (a, b) in enumerate(PASSES):
                    mm = nc.tensor.matmul(dst, lhs(a), rhs(b), start=first and n == 0,
                                          stop=last and n == len(PASSES) - 1)
                return mm

            def block_q0():
                for t in range(DT):
                    pe.wait_ge(*tile_count(x0_tile_ready, xt_ready, t))
                    for c in range(CT):
                        if t % HT == 0:
                            pe.wait_ge(w_ready, CT * (t // HT) + c + 1)
                        mm = product(bank[c][:], lambda a: a_w[:, a, t, P * c:P * (c + 1)],
                                     lambda b: a_xt[:, b, t, :], t == 0, t == DT - 1)
                        if t == DT - 1:
                            mm.then_inc(q_done, 1)
                    if t == HT - 1:
                        mm.then_inc(q_half, 1)

            def block_q(k):
                for half in range(2):
                    pe.wait_ge(xt_ready, k * 2 + half + 1)
                    for c in range(CT):
                        if half == 0:
                            pe.wait_ge(q_ready, (k - 1) * CT + c + 1)
                        tiles = range(DT // 2 * half, DT // 2 * (half + 1))
                        for t in tiles:
                            mm = product(bank[c][:], lambda a: a_w[:, a, t, P * c:P * (c + 1)],
                                         lambda b: a_xt[:, b, t, :], t == 0, t == DT - 1)
                        if half == 1:
                            mm.then_inc(q_done, 1)
                    if half == 0:
                        mm.then_inc(q_half, 1)

            block_q0()
            with pe.Fori(1, NBLOCKS) as k:
                block_q(k)

            def scores(unit, j, q=b_q):
                for t in range(CT):
                    mm = product(bank[j][:], lambda a: q[:, t, a, :], lambda b: b_mt[:, j, b, t, :],
                                 t == 0, t == CT - 1)
                mm.then_inc(s_done, 1)

            def step_pe(i, next_mt=None, own_mn=None, softmax=True, am_before=True, before_av=None, q=b_q):
                if softmax:
                    if q is b_q1:
                        pe.wait_ge(q1_loaded, 16)
                    else:
                        pe.wait_ge(uq_loaded, (i + 1) * 16)
                    for j in range(MB):
                        pe.wait_ge(exp_done, i * MB + j + 1)
                        if next_mt is not None:
                            pe.wait_ge(mt_ready, next_mt * MTS + HPJ * (j + 1))
                        scores(i + 1, j, q)
                if before_av is not None:
                    before_av()
                if am_before:
                    pe.wait_ge(am_ready, i)
                for g in range(MB):
                    pe.wait_ge(pt_ready, i * MB + g + 1)
                    if own_mn is not None:
                        pe.wait_ge(mn_ready, own_mn * MB + g + 1)
                    for s in range(TPB):
                        m = TPB * g + s
                        mm = product(ps_am[:], lambda a: b_pt[:, a, m, :], lambda b: b_mn[:, g, b, s, :],
                                     m == 0, m == MB * TPB - 1)
                    mm.then_inc(av_done, 1)

            pe.wait_ge(uq_loaded, 16)
            for j in range(MB):
                pe.wait_ge(q_ready, CT * (NBLOCKS - 1) + j + 1)
                pe.wait_ge(mt_ready, HPJ * (j + 1))
                scores(0, j)
            step_pe(0, own_mn=0, am_before=False, q=b_q1)

            with pe.Fori(0, NB - 1) as b:
                with pe.Fori(1, 7) as u:
                    step_pe(b * UPB + u)
                step_pe(b * UPB + 7, next_mt=b + 1)
                step_pe(b * UPB + 8, own_mn=b + 1)
            LB = (NB - 1) * UPB
            with pe.Fori(1, 7) as u:
                step_pe(LB + u)

            def x_tile(a, t, first):
                return (c_xl0 if first and a == LO and t < WG1_EARLY else c_xt[a])[:, P * t:P * (t + 1)]

            def gate_x(tiles, first=False):
                for t in tiles:
                    if first:
                        pe.wait_ge(wg1_ready, t + 1)
                    for h in range(DH):
                        mm = product(ps_z[h][:], lambda a: x_tile(a, t, first),
                                     lambda b: c_wg1[:, t, b, BANK * h:BANK * (h + 1)], t == 0, False)
                return mm

            def gate_x_early():
                pe.wait_ge(exp_done, NUNIT * MB)
                pe.wait_ge(cx0_early_ready, 1)
                gate_x(range(WG1_EARLY), first=True)

            step_pe(LB + 7, softmax=False, before_av=gate_x_early)

            def am_tile(a, t):
                return c_at[a][:, P * t:P * (t + 1)]

            def unit_c(k, first=False):
                pe.wait_ge(cx_ready, k + 1)
                if first:
                    gate_x(range(WG1_EARLY, DT), first=True).then_inc(cx_used, 1)
                else:
                    pe.wait_ge(z_biased, k * DH)
                    gate_x(range(DT)).then_inc(cx_used, 1)
                pe.wait_ge(ca_ready, k + 1)
                if first:
                    pe.wait_ge(wcm_ready, CT)
                for h in range(DH):
                    for t in range(CT):
                        mm = product(ps_z[h][:], lambda a: am_tile(a, t),
                                     lambda b: c_wc[:, t, b, BANK * h:BANK * (h + 1)], False, t == CT - 1)
                    mm.then_inc(z_done, 1)
                if first:
                    pe.wait_ge(wcm_ready, 2 * CT)
                else:
                    pe.wait_ge(mul_done, k * DH)
                for h in range(DH):
                    for t in range(CT):
                        mm = product(ps_c[h][:], lambda a: am_tile(a, t),
                                     lambda b: c_wm[:, t, b, BANK * h:BANK * (h + 1)], t == 0, t == CT - 1)
                    mm.then_inc(c_done, 1)

            unit_c(0, first=True)
            with pe.Fori(1, NUNIT) as k:
                unit_c(k)


_INS = ["x", "ctx_1024", "L0_xattn_W_mem", "L0_xattn_W_gate", "L0_xattn_b_gate", "L0_xattn_norm_w"]


def kernel(**inputs):
    import numpy as _np
    import concourse.bacc as _bacc
    from concourse import mybir as _mybir
    from concourse.bass_utils import run_bass_kernel_spmd as _run

    nc = _bacc.Bacc("TRN2", target_bir_lowering=False, num_devices=1)
    arrays, args = {}, []
    for name in _INS:
        a = _np.ascontiguousarray(inputs[name])
        arrays[f"in_{name}"] = a
        args.append(nc.dram_tensor(f"in_{name}", a.shape, _mybir.dt.from_np(a.dtype), kind="ExternalInput").ap())
    shape = inputs["x"].shape
    out = nc.dram_tensor("out", shape, _mybir.dt.float32, kind="ExternalOutput").ap()
    build(nc, *args, out)
    r = _run(nc, [arrays], core_ids=[0])
    return r.results[0]["out"]
```
